# Optimizing a Trainium2 kernel written in Bass

```python
import numpy as np
import jax
import jax.numpy as jnp

def _softmax(x, axis=-1):
    return jax.nn.softmax(x, axis=axis)

def _gelu(x):
    return jax.nn.gelu(x, approximate=True)

def _silu(x):
    return jax.nn.silu(x)

def _sigmoid(x):
    return jax.nn.sigmoid(x)

def _layernorm(x, axis=-1, eps=1e-05):
    m = jnp.mean(x, axis=axis, keepdims=True)
    v = jnp.var(x, axis=axis, keepdims=True)
    return (x - m) / jnp.sqrt(v + eps)

def _scatter_add(tgt, idx, src, axis=0):
    return tgt.at[idx].add(src)

def _segment_sum(src, seg, n):
    return jax.ops.segment_sum(src, seg, n)
kernel_name = 'mk_dlrm_tower_d1_rec_r8_4e9ac8'

def setup_inputs(seed: int=0):
    np.random.seed(seed)
    _w = jnp.asarray

    def _rec_inputs():
        import jax
        import jax.numpy as jnp
        _tk = jax.random.key(seed)
        dense_ctx = jax.random.normal(jax.random.fold_in(_tk, 190), (2048, 16), jnp.float32)
        ids = jnp.stack([jax.random.randint(jax.random.fold_in(_tk, 200 + f), (2048,), 0, v, jnp.int32) for f, v in enumerate([1250, 1250, 12500, 1250, 125000, 1000, 1250, 1250, 125000, 1250, 1250, 1250, 1000, 1250, 1250, 12500, 1000, 12500, 1250, 12500, 1250, 1250, 12500, 1250, 12500, 125000, 12500, 125000, 125000, 1000, 12500, 1250, 1000, 1250, 125000, 12500, 1000, 1250, 1250])], axis=1)
        tbl_0 = 0.05 * jax.random.normal(jax.random.fold_in(_tk, 500 + 0), (1250, 16), jnp.float32)
        tbl_1 = 0.05 * jax.random.normal(jax.random.fold_in(_tk, 500 + 1), (1250, 16), jnp.float32)
        tbl_2 = 0.05 * jax.random.normal(jax.random.fold_in(_tk, 500 + 2), (12500, 16), jnp.float32)
        tbl_3 = 0.05 * jax.random.normal(jax.random.fold_in(_tk, 500 + 3), (1250, 16), jnp.float32)
        tbl_4 = 0.05 * jax.random.normal(jax.random.fold_in(_tk, 500 + 4), (125000, 16), jnp.float32)
        tbl_5 = 0.05 * jax.random.normal(jax.random.fold_in(_tk, 500 + 5), (1000, 16), jnp.float32)
        tbl_6 = 0.05 * jax.random.normal(jax.random.fold_in(_tk, 500 + 6), (1250, 16), jnp.float32)
        tbl_7 = 0.05 * jax.random.normal(jax.random.fold_in(_tk, 500 + 7), (1250, 16), jnp.float32)
        tbl_8 = 0.05 * jax.random.normal(jax.random.fold_in(_tk, 500 + 8), (125000, 16), jnp.float32)
        tbl_9 = 0.05 * jax.random.normal(jax.random.fold_in(_tk, 500 + 9), (1250, 16), jnp.float32)
        tbl_10 = 0.05 * jax.random.normal(jax.random.fold_in(_tk, 500 + 10), (1250, 16), jnp.float32)
        tbl_11 = 0.05 * jax.random.normal(jax.random.fold_in(_tk, 500 + 11), (1250, 16), jnp.float32)
        tbl_12 = 0.05 * jax.random.normal(jax.random.fold_in(_tk, 500 + 12), (1000, 16), jnp.float32)
        tbl_13 = 0.05 * jax.random.normal(jax.random.fold_in(_tk, 500 + 13), (1250, 16), jnp.float32)
        tbl_14 = 0.05 * jax.random.normal(jax.random.fold_in(_tk, 500 + 14), (1250, 16), jnp.float32)
        tbl_15 = 0.05 * jax.random.normal(jax.random.fold_in(_tk, 500 + 15), (12500, 16), jnp.float32)
        tbl_16 = 0.05 * jax.random.normal(jax.random.fold_in(_tk, 500 + 16), (1000, 16), jnp.float32)
        tbl_17 = 0.05 * jax.random.normal(jax.random.fold_in(_tk, 500 + 17), (12500, 16), jnp.float32)
        tbl_18 = 0.05 * jax.random.normal(jax.random.fold_in(_tk, 500 + 18), (1250, 16), jnp.float32)
        tbl_19 = 0.05 * jax.random.normal(jax.random.fold_in(_tk, 500 + 19), (12500, 16), jnp.float32)
        tbl_20 = 0.05 * jax.random.normal(jax.random.fold_in(_tk, 500 + 20), (1250, 16), jnp.float32)
        tbl_21 = 0.05 * jax.random.normal(jax.random.fold_in(_tk, 500 + 21), (1250, 16), jnp.float32)
        tbl_22 = 0.05 * jax.random.normal(jax.random.fold_in(_tk, 500 + 22), (12500, 16), jnp.float32)
        tbl_23 = 0.05 * jax.random.normal(jax.random.fold_in(_tk, 500 + 23), (1250, 16), jnp.float32)
        tbl_24 = 0.05 * jax.random.normal(jax.random.fold_in(_tk, 500 + 24), (12500, 16), jnp.float32)
        tbl_25 = 0.05 * jax.random.normal(jax.random.fold_in(_tk, 500 + 25), (125000, 16), jnp.float32)
        tbl_26 = 0.05 * jax.random.normal(jax.random.fold_in(_tk, 500 + 26), (12500, 16), jnp.float32)
        tbl_27 = 0.05 * jax.random.normal(jax.random.fold_in(_tk, 500 + 27), (125000, 16), jnp.float32)
        tbl_28 = 0.05 * jax.random.normal(jax.random.fold_in(_tk, 500 + 28), (125000, 16), jnp.float32)
        tbl_29 = 0.05 * jax.random.normal(jax.random.fold_in(_tk, 500 + 29), (1000, 16), jnp.float32)
        tbl_30 = 0.05 * jax.random.normal(jax.random.fold_in(_tk, 500 + 30), (12500, 16), jnp.float32)
        tbl_31 = 0.05 * jax.random.normal(jax.random.fold_in(_tk, 500 + 31), (1250, 16), jnp.float32)
        tbl_32 = 0.05 * jax.random.normal(jax.random.fold_in(_tk, 500 + 32), (1000, 16), jnp.float32)
        tbl_33 = 0.05 * jax.random.normal(jax.random.fold_in(_tk, 500 + 33), (1250, 16), jnp.float32)
        tbl_34 = 0.05 * jax.random.normal(jax.random.fold_in(_tk, 500 + 34), (125000, 16), jnp.float32)
        tbl_35 = 0.05 * jax.random.normal(jax.random.fold_in(_tk, 500 + 35), (12500, 16), jnp.float32)
        tbl_36 = 0.05 * jax.random.normal(jax.random.fold_in(_tk, 500 + 36), (1000, 16), jnp.float32)
        tbl_37 = 0.05 * jax.random.normal(jax.random.fold_in(_tk, 500 + 37), (1250, 16), jnp.float32)
        tbl_38 = 0.05 * jax.random.normal(jax.random.fold_in(_tk, 500 + 38), (1250, 16), jnp.float32)
        _rk = jax.random.fold_in(_tk, 7)
        W_top1 = 0.0606339 * jax.random.normal(jax.random.fold_in(_tk, 801), (272, 512), jnp.float32)
        W_top2 = 0.0441942 * jax.random.normal(jax.random.fold_in(_tk, 802), (512, 256), jnp.float32)
        W_top3 = 0.0625 * jax.random.normal(jax.random.fold_in(_tk, 803), (256, 1), jnp.float32)
        b_top1 = jnp.zeros((512,), jnp.float32)
        b_top2 = jnp.zeros((256,), jnp.float32)
        return (dense_ctx, ids, tbl_0, tbl_1, tbl_2, tbl_3, tbl_4, tbl_5, tbl_6, tbl_7, tbl_8, tbl_9, tbl_10, tbl_11, tbl_12, tbl_13, tbl_14, tbl_15, tbl_16, tbl_17, tbl_18, tbl_19, tbl_20, tbl_21, tbl_22, tbl_23, tbl_24, tbl_25, tbl_26, tbl_27, tbl_28, tbl_29, tbl_30, tbl_31, tbl_32, tbl_33, tbl_34, tbl_35, tbl_36, tbl_37, tbl_38, W_top1, b_top1, W_top2, b_top2, W_top3)
    dense_ctx, ids, tbl_0, tbl_1, tbl_2, tbl_3, tbl_4, tbl_5, tbl_6, tbl_7, tbl_8, tbl_9, tbl_10, tbl_11, tbl_12, tbl_13, tbl_14, tbl_15, tbl_16, tbl_17, tbl_18, tbl_19, tbl_20, tbl_21, tbl_22, tbl_23, tbl_24, tbl_25, tbl_26, tbl_27, tbl_28, tbl_29, tbl_30, tbl_31, tbl_32, tbl_33, tbl_34, tbl_35, tbl_36, tbl_37, tbl_38, W_top1, b_top1, W_top2, b_top2, W_top3 = _rec_inputs()

    def _L0_rec_setup():
        import jax, jax.numpy as jnp
        import numpy as np
        B, F0, D = (256, 39, 16)
        LAYER_SIZES = [128, 128, 128]
        key = jax.random.key(seed)
        ks = jax.random.split(key, 1 + 2 * len(LAYER_SIZES))
        inputs = jax.random.normal(ks[0], (B, F0, D), dtype=jnp.float32)
        out = {'inputs': inputs}
        field_nums = [F0]
        for i, size in enumerate(LAYER_SIZES):
            fk = field_nums[-1]
            fan_in = F0 * fk
            scale = np.sqrt(2.0 / (fan_in + size)).astype(np.float32)
            out[f'w{i}'] = jax.random.normal(ks[1 + 2 * i], (F0, fk, size), dtype=jnp.float32) * scale
            out[f'b{i}'] = jnp.zeros((size,), dtype=jnp.float32)
            field_nums.append(size // 2)
        return out
    _L0_rec_all = _L0_rec_setup()
    _L0_rec_in = {k: v for k, v in _L0_rec_all.items() if k in ('w0', 'w1', 'w2', 'b0', 'b1', 'b2')}
    del _L0_rec_all
    return {'dense_ctx': dense_ctx, 'ids': ids, 'tbl_0': tbl_0, 'tbl_1': tbl_1, 'tbl_2': tbl_2, 'tbl_3': tbl_3, 'tbl_4': tbl_4, 'tbl_5': tbl_5, 'tbl_6': tbl_6, 'tbl_7': tbl_7, 'tbl_8': tbl_8, 'tbl_9': tbl_9, 'tbl_10': tbl_10, 'tbl_11': tbl_11, 'tbl_12': tbl_12, 'tbl_13': tbl_13, 'tbl_14': tbl_14, 'tbl_15': tbl_15, 'tbl_16': tbl_16, 'tbl_17': tbl_17, 'tbl_18': tbl_18, 'tbl_19': tbl_19, 'tbl_20': tbl_20, 'tbl_21': tbl_21, 'tbl_22': tbl_22, 'tbl_23': tbl_23, 'tbl_24': tbl_24, 'tbl_25': tbl_25, 'tbl_26': tbl_26, 'tbl_27': tbl_27, 'tbl_28': tbl_28, 'tbl_29': tbl_29, 'tbl_30': tbl_30, 'tbl_31': tbl_31, 'tbl_32': tbl_32, 'tbl_33': tbl_33, 'tbl_34': tbl_34, 'tbl_35': tbl_35, 'tbl_36': tbl_36, 'tbl_37': tbl_37, 'tbl_38': tbl_38, 'W_top1': W_top1, 'b_top1': b_top1, 'W_top2': W_top2, 'b_top2': b_top2, 'W_top3': W_top3, 'L0_rec_w0': _L0_rec_in['w0'], 'L0_rec_w1': _L0_rec_in['w1'], 'L0_rec_w2': _L0_rec_in['w2'], 'L0_rec_b0': _L0_rec_in['b0'], 'L0_rec_b1': _L0_rec_in['b1'], 'L0_rec_b2': _L0_rec_in['b2']}

def reference(dense_ctx, ids, tbl_0, tbl_1, tbl_2, tbl_3, tbl_4, tbl_5, tbl_6, tbl_7, tbl_8, tbl_9, tbl_10, tbl_11, tbl_12, tbl_13, tbl_14, tbl_15, tbl_16, tbl_17, tbl_18, tbl_19, tbl_20, tbl_21, tbl_22, tbl_23, tbl_24, tbl_25, tbl_26, tbl_27, tbl_28, tbl_29, tbl_30, tbl_31, tbl_32, tbl_33, tbl_34, tbl_35, tbl_36, tbl_37, tbl_38, W_top1, b_top1, W_top2, b_top2, W_top3, L0_rec_w0, L0_rec_w1, L0_rec_w2, L0_rec_b0, L0_rec_b1, L0_rec_b2):
    import jax
    import jax.numpy as jnp

    def _L0_rec_ref(inputs, w0, w1, w2, b0, b1, b2):
        import jax, jax.numpy as jnp
        import numpy as np
        B, F0, D = (256, 39, 16)
        LAYER_SIZES = [128, 128, 128]
        x0 = inputs
        xk = inputs
        params = [(w0, b0), (w1, b1), (w2, b2)]
        n_layers = len(params)
        direct = []
        for idx, (W, b) in enumerate(params):
            z = jnp.einsum('bhd,bkd,hks->bsd', x0, xk, W) + b[None, :, None]
            z = jax.nn.relu(z)
            if idx != n_layers - 1:
                half = z.shape[1] // 2
                xk = z[:, :half, :]
                direct.append(z[:, half:, :])
            else:
                direct.append(z)
        logit = jnp.sum(jnp.concatenate(direct, axis=1), axis=-1)
        return logit
    e = jnp.stack([tbl_0[ids[:, 0]], tbl_1[ids[:, 1]], tbl_2[ids[:, 2]], tbl_3[ids[:, 3]], tbl_4[ids[:, 4]], tbl_5[ids[:, 5]], tbl_6[ids[:, 6]], tbl_7[ids[:, 7]], tbl_8[ids[:, 8]], tbl_9[ids[:, 9]], tbl_10[ids[:, 10]], tbl_11[ids[:, 11]], tbl_12[ids[:, 12]], tbl_13[ids[:, 13]], tbl_14[ids[:, 14]], tbl_15[ids[:, 15]], tbl_16[ids[:, 16]], tbl_17[ids[:, 17]], tbl_18[ids[:, 18]], tbl_19[ids[:, 19]], tbl_20[ids[:, 20]], tbl_21[ids[:, 21]], tbl_22[ids[:, 22]], tbl_23[ids[:, 23]], tbl_24[ids[:, 24]], tbl_25[ids[:, 25]], tbl_26[ids[:, 26]], tbl_27[ids[:, 27]], tbl_28[ids[:, 28]], tbl_29[ids[:, 29]], tbl_30[ids[:, 30]], tbl_31[ids[:, 31]], tbl_32[ids[:, 32]], tbl_33[ids[:, 33]], tbl_34[ids[:, 34]], tbl_35[ids[:, 35]], tbl_36[ids[:, 36]], tbl_37[ids[:, 37]], tbl_38[ids[:, 38]]], axis=1)
    z = _L0_rec_ref(e, L0_rec_w0, L0_rec_w1, L0_rec_w2, L0_rec_b0, L0_rec_b1, L0_rec_b2)
    z = z.reshape(z.shape[0], -1)
    h = jnp.concatenate([z, dense_ctx], axis=1)
    h = jnp.maximum(h @ W_top1 + b_top1, 0.0)
    h = jnp.maximum(h @ W_top2 + b_top2, 0.0)
    y = h @ W_top3
    return y

_drawn_inputs = setup_inputs


def setup_inputs(seed=0):
    import zlib

    import numpy as np

    out = dict(_drawn_inputs(seed))
    spreads = {'b_top1': (0.0, 2.0),
     'b_top2': (0.0, 2.0),
     'L0_rec_b0': (0.0, 0.339),
     'L0_rec_b1': (0.0, 0.527),
     'L0_rec_b2': (0.0, 0.8)}
    factors = {'tbl_0': 8.0,
     'tbl_1': 8.0,
     'tbl_2': 8.0,
     'tbl_3': 8.0,
     'tbl_4': 8.0,
     'tbl_5': 8.0,
     'tbl_6': 8.0,
     'tbl_7': 8.0,
     'tbl_8': 8.0,
     'tbl_9': 8.0,
     'tbl_10': 8.0,
     'tbl_11': 8.0,
     'tbl_12': 8.0,
     'tbl_13': 8.0,
     'tbl_14': 8.0,
     'tbl_15': 8.0,
     'tbl_16': 8.0,
     'tbl_17': 8.0,
     'tbl_18': 8.0,
     'tbl_19': 8.0,
     'tbl_20': 8.0,
     'tbl_21': 8.0,
     'tbl_22': 8.0,
     'tbl_23': 8.0,
     'tbl_24': 8.0,
     'tbl_25': 8.0,
     'tbl_26': 8.0,
     'tbl_27': 8.0,
     'tbl_28': 8.0,
     'tbl_29': 8.0,
     'tbl_30': 8.0,
     'tbl_31': 8.0,
     'tbl_32': 8.0,
     'tbl_33': 8.0,
     'tbl_34': 8.0,
     'tbl_35': 8.0,
     'tbl_36': 8.0,
     'tbl_37': 8.0,
     'tbl_38': 8.0,
     'L0_rec_w0': 8.0,
     'L0_rec_w1': 6.25,
     'L0_rec_w2': 4.662,
     'dense_ctx': 8.0}
    for name, (base, spread) in spreads.items():
        noise = np.random.default_rng([zlib.crc32(name.encode()), seed]).standard_normal(out[name].shape)
        drawn = base * np.exp(spread * noise) if base else spread * noise
        out[name] = jnp.asarray(drawn.astype(out[name].dtype))
    for name, factor in factors.items():
        out[name] = (out[name] * factor).astype(out[name].dtype)
    return out
```

```python
from contextlib import ExitStack

import concourse.bass as bass
import concourse.mybir as mybir
import numpy as np

B, F, D = 2048, 39, 16
S, H = 128, 64
N = B * D
CB = 32
CN = CB * D
CHUNKS = B // CB
GB = 128
GATHERS = B // GB
PER_GATHER = GB // CB

SHIFTS = (F + 1) // 2
JT = 3
T0 = -(-SHIFTS // JT)
LAST0 = (SHIFTS - JT * (T0 - 1)) * F
XROWS = F + SHIFTS - 1
TK = -(-F // 2)

PAIR = 2
G0 = -(-T0 // PAIR)
GK = TK // PAIR
GC = G0 + 2 * GK
SLOTS = 6
assert GC % SLOTS == 0

T1, T2 = 512, 256
CTX = 16
MB = 512


def tower(nc, tables, ids, ctx_t, w0a, w0b, w1, w2, wt1, wt1c, wt2, cols, out):
    f32, i32 = mybir.dt.float32, mybir.dt.int32
    ALU, ACT, AX = mybir.AluOpType, mybir.ActivationFunctionType, mybir.AxisListType

    x0_dram = nc.dram_tensor("x0_rows", (XROWS, N), f32, kind="Internal").ap()

    with ExitStack() as stack:
        def sb(name, shape, dt=f32):
            return stack.enter_context(nc.sbuf_tensor(name, shape, dt))

        def bank(name, width=512):
            return stack.enter_context(nc.psum_tensor(name, [128, width], f32))

        def sem(name):
            return stack.enter_context(nc.semaphore(name))

        w0_sb = sb("w0_sb", [JT * F, T0, S])
        w0b_sb = sb("w0b_sb", [JT * F, T0, S])
        w1_sb = sb("w1_sb", [128, TK, S])
        w2_sb = sb("w2_sb", [128, TK, S])
        wt1_sb = sb("wt1_sb", [128, 2, T1])
        wt1c_sb = sb("wt1c_sb", [CTX, T1])
        wt2_sb = sb("wt2_sb", [128, T1 // 128, T2])
        cols_sb = sb("cols_sb", [128, 3 + T1 // 128 + 2 * (T2 // 128)])
        bias = [cols_sb[:, i:i + 1] for i in range(3)]
        bt1 = [cols_sb[:, 3 + i:4 + i] for i in range(4)]
        bt2 = [cols_sb[:, 7 + i:8 + i] for i in range(2)]
        wt3 = [cols_sb[:, 9 + i:10 + i] for i in range(2)]

        ids_sb = [sb(f"ids{i}", [GB, F], i32) for i in range(2)]
        rows_sb = [sb(f"rows{i}", [GB, F * D]) for i in range(2)]
        xh = [sb(f"xh{i}", [128, TK, CN]) for i in range(2)]
        xa = sb("xa", [JT * F, CN])
        xb = sb("xb", [JT * F, T0, CN])
        prod = sb("prod", [128, SLOTS, PAIR, CN])
        direct = sb("direct", [128, CN])
        last = sb("last", [128, CN])
        feats = sb("feats", [128, 2, B])
        ctx_sb = sb("ctx_sb", [CTX, B])
        ring = prod[:, :, :, :].rearrange("p s i n -> p (s i) n")
        h1 = ring[:, 0:T1 // 128, :]
        h2 = ring[:, 4:4 + T2 // 128, :]
        y_sb = ring[0:1, 6:6 + B // MB, :]

        z = [bank(f"z{i}") for i in range(3)]
        xk = [bank("x1"), bank("x2")]
        mlp = [bank(f"mlp{i}") for i in range(3)]

        weights_loaded = sem("weights_loaded")
        w0_loaded = sem("w0_loaded")
        w0_summed = sem("w0_summed")
        pads_cleared = sem("pads_cleared")
        ids_loaded = [sem(f"ids_loaded{i}") for i in range(2)]
        gathered = [sem(f"gathered{i}") for i in range(2)]
        gather_begun = sem("gather_begun")
        stored = [sem(f"stored{i}") for i in range(2)]
        xh_loaded = [sem(f"xh_loaded{i}") for i in range(2)]
        x0_loaded = sem("x0_loaded")
        products_ready = sem("products_ready")
        products_used = sem("products_used")
        relu_done = [sem(f"relu{i}_done") for i in range(3)]
        direct_summed = sem("direct_summed")
        last_summed = sem("last_summed")
        hidden1_done = sem("hidden1_done")
        hidden1_relu = sem("hidden1_relu")
        hidden2_done = sem("hidden2_done")
        hidden2_relu = sem("hidden2_relu")
        y_done = sem("y_done")
        y_copied = sem("y_copied")
        y_stored = sem("y_stored")

        def first_group(stage, c):
            if stage == 0:
                return 0 if isinstance(c, int) and c == 0 else GC * (c - 1) + G0 + GK
            return GC * c + G0 + (0 if stage == 1 else GK + G0)

        def groups_before(stage, c):
            g = first_group(stage, c)
            return g - G0 if stage == 2 and isinstance(c, int) and c == CHUNKS - 1 else g

        def tiles_of(stage):
            total = T0 if stage == 0 else TK
            return [range(t, min(t + PAIR, total)) for t in range(0, total, PAIR)]

        def slot(stage, c, g):
            return (groups_before(stage, c if isinstance(c, int) else 1) + g) % SLOTS

        def over_chunks(engine, step):
            step(0)
            step(1)
            with engine.Fori(1, CHUNKS // 2 - 1) as i:
                step(2 * i, 0)
                step(2 * i + 1, 1)
            step(CHUNKS - 2)
            step(CHUNKS - 1)

        block = stack.enter_context(nc.Block())

        @block.sync
        def _(sp):
            def load_ids(t, p):
                sp.dma_start(ids_sb[p][:, :], ids[bass.ds(t * GB, GB), :]).then_inc(ids_loaded[p], 16)

            def store_rows(t, p, uses):
                sp.wait_ge(gathered[p], uses * F * 16)
                src = rows_sb[p][:, :].rearrange("b (f d) -> b f d", d=D)
                dst = x0_dram.rearrange("f (b d) -> b f d", d=D)[bass.ds(t * GB, GB), :, :]
                sp.dma_start(dst[:, 0:F, :], src).then_inc(stored[p], 16)
                sp.dma_start(dst[:, F:XROWS, :], src[:, 0:XROWS - F, :]).then_inc(stored[p], 16)

            def load_pairs(c):
                col = x0_dram[:, bass.ds(c * CN, CN)]
                for jj in range(JT):
                    n = (SHIFTS - jj + JT - 1) // JT
                    at = slice(jj * F, (jj + 1) * F)
                    sp.dma_start(xa[at, :], col[0:F, :]).then_inc(x0_loaded, 16)
                    step = col.ap[0][0]
                    shifted = bass.AP(tensor=col.tensor, offset=col.offset + jj * step,
                                      ap=[[step, F], [JT * step, n], [1, CN]])
                    sp.dma_start(xb[at, 0:n, :], shifted).then_inc(x0_loaded, 16)

            def load_fields(c, p):
                col = x0_dram[:, bass.ds(c * CN, CN)]
                step = col.ap[0][0]
                for hh in range(2):
                    n = (F + 1 - hh) // 2
                    spread = bass.AP(tensor=col.tensor, offset=col.offset + hh * step,
                                     ap=[[0, H], [2 * step, n], [1, CN]])
                    sp.dma_start(xh[p][hh * H:(hh + 1) * H, 0:n, :], spread).then_inc(xh_loaded[p], 16)

            load_ids(0, 0)
            load_ids(1, 1)
            for dst, src in ((w0_sb, w0a), (w0b_sb, w0b)):
                sp.dma_start(dst[:, :, :], src).then_inc(w0_loaded, 16)
            for dst, src in ((w1_sb, w1), (w2_sb, w2), (wt1_sb, wt1), (wt2_sb, wt2)):
                sp.dma_start(dst[:, :, :], src).then_inc(weights_loaded, 16)
            for dst, src in ((wt1c_sb, wt1c), (cols_sb, cols), (ctx_sb, ctx_t)):
                sp.dma_start(dst[:, :], src).then_inc(weights_loaded, 16)

            def block_of_chunks(t, p, uses, peeled=None):
                final = peeled == "last"
                if not final:
                    store_rows(t + 1, 1 - p, uses if p == 0 else uses + 1)
                if peeled != "last" and peeled != "second_last":
                    sp.wait_ge(gathered[p], uses * F * 16)
                    load_ids(t + 2, p)
                for q in range(PER_GATHER):
                    c = PER_GATHER * t + q
                    sp.wait_ge(stored[p], uses * 32)
                    if not (peeled == "first" and q == 0):
                        sp.wait_ge(products_ready, first_group(0, c) - GC + G0
                                   if not isinstance(c, int) or c > 1 else G0)
                    load_pairs(c)
                    if not (peeled == "first" and q < 2):
                        sp.wait_ge(products_ready, first_group(1, c - 1))
                    load_fields(c, q % 2)

            sp.wait_ge(pads_cleared, 2)
            store_rows(0, 0, 1)
            block_of_chunks(0, 0, 1, "first")
            block_of_chunks(1, 1, 1)
            with sp.Fori(1, GATHERS // 2 - 1) as i:
                block_of_chunks(2 * i, 0, i + 1)
                block_of_chunks(2 * i + 1, 1, i + 1)
            block_of_chunks(GATHERS - 2, 0, GATHERS // 2, "second_last")
            block_of_chunks(GATHERS - 1, 1, GATHERS // 2, "last")
            sp.wait_ge(y_copied, B // MB)
            sp.dma_start(out.rearrange("(m b) o -> o m b", b=MB), y_sb).then_inc(y_stored, 16)
            sp.wait_ge(y_stored, 16)

        @block.gpsimd
        def _(pool):
            for p in range(2):
                pool.memset(xh[p][H:128, TK - 1, :], 0.0).then_inc(pads_cleared, 1)

            def gather(p, uses, first=False):
                pool.wait_ge(ids_loaded[p], uses * 16)
                if not first:
                    pool.wait_ge(stored[p], (uses - 1) * 32)
                pool.sem_inc(gather_begun, 1)
                for f in range(F):
                    pool.indirect_dma_start(
                        rows_sb[p][:, f * D:(f + 1) * D], None, tables[f],
                        bass.IndirectOffsetOnAxis(ap=ids_sb[p][:, f:f + 1], axis=0),
                    ).then_inc(gathered[p], 16)

            gather(0, 1, True)
            gather(1, 1, True)
            with pool.Fori(1, GATHERS // 2) as i:
                gather(0, i + 1)
                gather(1, i + 1)

        @block.vector
        def _(dve):
            def products(stage, c, in0, in1):
                for g, tiles in enumerate(tiles_of(stage)):
                    before = groups_before(stage, c) + g
                    if not isinstance(before, int) or before >= SLOTS:
                        dve.wait_ge(products_used, before - SLOTS + 1)
                    n = len(tiles)
                    rows = 128 if stage else (LAST0 if tiles[0] == T0 - 1 else JT * F)
                    t = slice(tiles[0], tiles[0] + n)
                    dve.tensor_tensor(
                        prod[0:rows, slot(stage, c, g), 0:n, :], in0[0:rows, t, :],
                        in1[0:rows, :].unsqueeze(1).broadcast_to([rows, n, CN]), ALU.mult,
                    ).then_inc(products_ready, 1)
                    yield g

            def sum_last(c):
                dve.wait_ge(relu_done[2], c + 1)
                dve.tensor_reduce(feats[:, 1, bass.ds(c * CB, CB)],
                                  last[:, :].rearrange("p (b d) -> p b d", d=D),
                                  axis=AX.X, op=ALU.add).then_inc(last_summed, 1)

            def sum_direct(c):
                dve.wait_ge(relu_done[1], 3 * c + 3)
                dve.tensor_reduce(feats[:, 0, bass.ds(c * CB, CB)],
                                  direct[:, :].rearrange("p (b d) -> p b d", d=D),
                                  axis=AX.X, op=ALU.add).then_inc(direct_summed, 1)

            def layer0(c):
                dve.wait_ge(x0_loaded, (c + 1) * 2 * JT * 16)
                for _ in products(0, c, xb, xa):
                    pass

            def chunk(c, p=None):
                p = c % 2 if p is None else p
                known = isinstance(c, int)
                uses = c // 2 + 1 if known else None
                if known:
                    dve.wait_ge(xh_loaded[p], 32 * uses)
                else:
                    dve.wait_ge(xh_loaded[p], 16 * c + (32 if p == 0 else 16))
                dve.wait_ge(relu_done[0], 3 * c + 2)
                for g in products(1, c, xh[p], xk[0]):
                    if g == 2 and not (known and c == 0):
                        sum_last(c - 1)
                if not (known and c == CHUNKS - 1):
                    layer0(c + 1)
                dve.wait_ge(relu_done[1], 3 * c + 2)
                for g in products(2, c, xh[p], xk[1]):
                    if g == 2:
                        sum_direct(c)

            dve.wait_ge(w0_loaded, 32)
            dve.tensor_tensor(w0_sb[:, :, :], w0_sb[:, :, :], w0b_sb[:, :, :],
                              ALU.add).then_inc(w0_summed, 1)
            dve.wait_ge(pads_cleared, 2)
            layer0(0)
            over_chunks(dve, chunk)
            sum_last(CHUNKS - 1)
            for m in range(B // MB):
                dve.wait_ge(y_done, m + 1)
                dve.tensor_copy(y_sb[:, m, :], mlp[2][0:1, :]).then_inc(y_copied, 1)

        @block.tensor
        def _(pe):
            def contract(stage, c, weights):
                known = isinstance(c, int)
                if not (known and c == 0):
                    pe.wait_ge(relu_done[stage], (1 if stage == 2 else 3) * c)
                total = T0 if stage == 0 else TK
                for g, tiles in enumerate(tiles_of(stage)):
                    pe.wait_ge(products_ready, groups_before(stage, c) + g + 1)
                    for i, t in enumerate(tiles):
                        rows = 128 if stage else (LAST0 if t == T0 - 1 else JT * F)
                        mm = pe.matmul(z[stage][:, :], weights[0:rows, t, :],
                                       prod[0:rows, slot(stage, c, g), i, :],
                                       start=t == 0, stop=t == total - 1)
                        if i == len(tiles) - 1:
                            mm.then_inc(products_used, 1)

            def chunk(c, p=None):
                contract(1, c, w1_sb)
                if not (isinstance(c, int) and c == CHUNKS - 1):
                    contract(0, c + 1, w0_sb)
                contract(2, c, w2_sb)

            pe.wait_ge(w0_summed, 1)
            contract(0, 0, w0_sb)
            pe.wait_ge(weights_loaded, 7 * 16)
            over_chunks(pe, chunk)

            pe.wait_ge(direct_summed, CHUNKS)
            pe.wait_ge(last_summed, CHUNKS)
            n1 = T1 // 128
            n2 = T2 // 128
            for m in range(B // MB):
                at = slice(m * MB, (m + 1) * MB)
                for j in range(n1):
                    k = n1 * m + j
                    if k >= 2:
                        pe.wait_ge(hidden1_relu, k - 1)
                    if m and j < 2:
                        pe.wait_ge(hidden2_relu, n2 * m - 1 + j)
                    js = slice(j * 128, (j + 1) * 128)
                    acc = mlp[k % 2][:, :]
                    pe.matmul(acc, wt1_sb[:, 0, js], feats[:, 0, at], start=True, stop=False)
                    pe.matmul(acc, wt1_sb[:, 1, js], feats[:, 1, at], start=False, stop=False)
                    pe.matmul(acc, wt1c_sb[:, js], ctx_sb[:, at], start=False,
                              stop=True).then_inc(hidden1_done, 1)
                pe.wait_ge(hidden1_relu, n1 * (m + 1))
                for j in range(n2):
                    js = slice(j * 128, (j + 1) * 128)
                    for i in range(n1):
                        mm = pe.matmul(mlp[j][:, :], wt2_sb[:, i, js], h1[:, i, :],
                                       start=i == 0, stop=i == n1 - 1)
                    mm.then_inc(hidden2_done, 1)
                pe.wait_ge(hidden2_relu, n2 * (m + 1))
                if m:
                    pe.wait_ge(y_copied, m)
                for i in range(n2):
                    mm = pe.matmul(mlp[2][0:1, :], wt3[i], h2[:, i, :], start=i == 0, stop=i == n2 - 1)
                mm.then_inc(y_done, 1)

        @block.scalar
        def _(act):
            def layer_out(stage, c):
                known = isinstance(c, int)
                ends = groups_before(stage, c) + (G0 if stage == 0 else GK)
                act.wait_ge(products_used, ends)
                if stage == 2:
                    if not (known and c == 0):
                        act.wait_ge(last_summed, c)
                    act.activation(last[:, :], z[2][:, :], ACT.Relu,
                                   bias=bias[2]).then_inc(relu_done[2], 1)
                    return
                if not (known and c == 0):
                    act.wait_ge(products_ready, groups_before(stage + 1, c) - GC + GK)
                feed = slice(0, H) if stage == 0 else slice(H, 128)
                leave = slice(H, 128) if stage == 0 else slice(0, H)
                for half in (slice(0, H), slice(H, 128)):
                    act.activation(xk[stage][half, :], z[stage][feed, :], ACT.Relu,
                                   bias=bias[stage][feed, :]).then_inc(relu_done[stage], 1)
                if stage == 0 and not (known and c == 0):
                    act.wait_ge(direct_summed, c)
                act.activation(direct[leave, :], z[stage][leave, :], ACT.Relu,
                               bias=bias[stage][leave, :]).then_inc(relu_done[stage], 1)

            def chunk(c, p=None):
                layer_out(1, c)
                if not (isinstance(c, int) and c == CHUNKS - 1):
                    layer_out(0, c + 1)
                layer_out(2, c)

            act.wait_ge(weights_loaded, 7 * 16)
            layer_out(0, 0)
            over_chunks(act, chunk)

            n1 = T1 // 128
            n2 = T2 // 128
            for m in range(B // MB):
                for j in range(n1):
                    k = n1 * m + j
                    act.wait_ge(hidden1_done, k + 1)
                    if m and j == 0:
                        act.wait_ge(hidden2_done, n2 * m)
                    act.activation(h1[:, j, :], mlp[k % 2][:, :], ACT.Relu,
                                   bias=bt1[j]).then_inc(hidden1_relu, 1)
                for j in range(n2):
                    act.wait_ge(hidden2_done, n2 * m + j + 1)
                    if m and j == 0:
                        act.wait_ge(y_done, m)
                    act.activation(h2[:, j, :], mlp[j][:, :], ACT.Relu,
                                   bias=bt2[j]).then_inc(hidden2_relu, 1)


def kernel(**inputs):
    import concourse.bacc as bacc
    from concourse.bass_utils import run_bass_kernel_spmd

    a = {k: np.ascontiguousarray(np.asarray(v)) for k, v in inputs.items()}

    w0 = a["L0_rec_w0"]
    w0a = np.zeros((JT * F, T0, S), w0.dtype)
    w0b = np.zeros((JT * F, T0, S), w0.dtype)
    first = np.arange(F)
    for j in range(SHIFTS):
        second = (first + j) % F
        at = slice(j % JT * F, (j % JT + 1) * F)
        w0a[at, j // JT] = w0[first, second]
        if j:
            w0b[at, j // JT] = w0[second, first]

    def by_fields(w):
        tiles = np.zeros((2 * TK, H, w.shape[2]), w.dtype)
        tiles[:F] = w
        return np.ascontiguousarray(tiles.reshape(TK, 2 * H, w.shape[2]).transpose(1, 0, 2))

    def by_128(m):
        return np.ascontiguousarray(m.reshape(-1, 128, m.shape[1]).transpose(1, 0, 2))

    turned = np.r_[H:S, 0:H]
    wt1 = a["W_top1"]
    cols = np.concatenate(
        [a["L0_rec_b0"].reshape(1, S), a["L0_rec_b1"][turned].reshape(1, S),
         a["L0_rec_b2"].reshape(1, S), a["b_top1"].reshape(-1, 128), a["b_top2"].reshape(-1, 128),
         a["W_top3"].reshape(-1, 128)]).T
    arrays = {
        "ids": a["ids"],
        "ctx_t": np.ascontiguousarray(a["dense_ctx"].T),
        "w0a": w0a, "w0b": w0b,
        "w1": by_fields(a["L0_rec_w1"][:, :, turned]),
        "w2": by_fields(a["L0_rec_w2"]),
        "wt1": by_128(np.concatenate([wt1[H:2 * H], wt1[0:H], wt1[2 * H:4 * H]])),
        "wt1c": np.ascontiguousarray(wt1[4 * H:]),
        "wt2": by_128(a["W_top2"]),
        "cols": np.ascontiguousarray(cols),
    }
    names = list(arrays)
    for f in range(F):
        arrays[f"tbl_{f}"] = a[f"tbl_{f}"]

    nc = bacc.Bacc("TRN2", target_bir_lowering=False, num_devices=1)
    dram = {k: nc.dram_tensor(k, v.shape, mybir.dt.from_np(v.dtype), kind="ExternalInput").ap()
            for k, v in arrays.items()}
    out = nc.dram_tensor("out", (B, 1), mybir.dt.float32, kind="ExternalOutput").ap()
    tower(nc, [dram[f"tbl_{f}"] for f in range(F)], *[dram[k] for k in names], out)
    r = run_bass_kernel_spmd(nc, [arrays], core_ids=[0])
    return r.results[0]["out"]
```

```python
from contextlib import ExitStack

import concourse.bass as bass
import concourse.mybir as mybir
import numpy as np

B, F, D = 2048, 39, 16
S, H = 128, 64
N = B * D
CB = 32
CN = CB * D
CHUNKS = B // CB
GB = 128
GATHERS = B // GB
PER_GATHER = GB // CB

SHIFTS = (F + 1) // 2
JT = 3
T0 = -(-SHIFTS // JT)
LAST0 = (SHIFTS - JT * (T0 - 1)) * F
XROWS = F + SHIFTS - 1
TK = -(-F // 2)

PAIR = 2
WHOLE, BY_POOL, BY_DVE = "whole", "low parts by GpSimd", "low parts by VectorE"
KINDS = {
    0: [BY_POOL, BY_DVE, BY_POOL, WHOLE],
    1: [WHOLE, BY_POOL, BY_DVE, BY_POOL, WHOLE, BY_POOL, WHOLE, BY_DVE, BY_POOL, WHOLE],
}
KINDS[2] = KINDS[1]
WHOLE_SLOTS, POOL_SLOTS, SPLIT_SLOTS = 3, 2, 3

AFTER, OUT2, XA, OUT0 = 5, 3, 2, 3
T1, T2 = 512, 256
CTX = 16
MB = 512

STAGED = {0: 0, 1: T0, 2: T0 + TK}
TURNED = T0 + 2 * TK
ALL_TILES = TURNED + T0


class Group:

    def __init__(self, stage, chunk, g, counts):
        total = T0 if stage == 0 else TK
        self.stage, self.chunk, self.g, self.kind = stage, chunk, g, KINDS[stage][g]
        self.tiles = range(PAIR * g, min(PAIR * (g + 1), total))
        self.ends_layer = self.tiles[-1] == total - 1
        self.rows = 128 if stage else (LAST0 if self.ends_layer else JT * F)
        self.split = self.kind != WHOLE
        self.n = counts["all"]
        self.k = counts["split"]
        self.of_kind = counts[self.kind]
        counts["all"] += 1
        counts["split"] += self.split
        counts[self.kind] += 1
        self.slot = self.of_kind % {WHOLE: WHOLE_SLOTS, BY_POOL: POOL_SLOTS, BY_DVE: 1}[self.kind]
        self.split_slot = self.k % SPLIT_SLOTS


def plan():
    counts = dict.fromkeys(("all", "split", WHOLE, BY_POOL, BY_DVE), 0)
    order = [(0, 0)]
    for c in range(CHUNKS):
        order += [(1, c)] + [(0, c + 1)] * (c + 1 < CHUNKS) + [(2, c)]
    return {(stage, c): [Group(stage, c, g, counts) for g in range(len(KINDS[stage]))]
            for stage, c in order}


PLAN = plan()
EVERY = [g for gs in PLAN.values() for g in gs]
SPLITS = [g for g in EVERY if g.split]
WHOLES = [g for g in EVERY if not g.split]
LIKE = 2
PER = {"all": sum(map(len, KINDS.values())),
       "split": sum(k != WHOLE for ks in KINDS.values() for k in ks),
       BY_POOL: sum(k == BY_POOL for ks in KINDS.values() for k in ks),
       BY_DVE: sum(k == BY_DVE for ks in KINDS.values() for k in ks)}
assert (PER["all"] - PER["split"]) % WHOLE_SLOTS == 0
assert PER[BY_POOL] % POOL_SLOTS == 0 and PER["split"] % SPLIT_SLOTS == 0

WHOLE_TILE, SPLIT_TILE = {}, {}
for _stage in range(3):
    for _group in PLAN[_stage, 0]:
        for _t in _group.tiles:
            _to = SPLIT_TILE if _group.split else WHOLE_TILE
            _to[_stage, _t] = len(_to)


def tower(nc, tables, ids, ctx_t, staged, wt1, wt1c, wt2, cols, out):
    f32, f32r, i32 = mybir.dt.float32, mybir.dt.float32r, mybir.dt.int32
    ALU, ACT, AX = mybir.AluOpType, mybir.ActivationFunctionType, mybir.AxisListType

    x0_dram = nc.dram_tensor("x0_rows", (XROWS, N), f32, kind="Internal").ap()

    with ExitStack() as stack:
        def sb(name, shape, dt=f32):
            return stack.enter_context(nc.sbuf_tensor(name, shape, dt))

        def bank(name, banks=1):
            return stack.enter_context(nc.psum_tensor(name, [128, banks * 512], f32))

        def sem(name):
            return stack.enter_context(nc.semaphore(name))

        w_whole = sb("w_whole", [128, len(WHOLE_TILE), S])
        w_high = sb("w_high", [128, len(SPLIT_TILE), S], f32r)
        w_low = sb("w_low", [128, len(SPLIT_TILE), S], f32r)
        cols_sb = sb("cols_sb", [128, 3 + T1 // 128 + 2 * (T2 // 128)])
        bias = [cols_sb[:, i:i + 1] for i in range(3)]
        bt1 = [cols_sb[:, 3 + i:4 + i] for i in range(4)]
        bt2 = [cols_sb[:, 7 + i:8 + i] for i in range(2)]
        wt3 = [cols_sb[:, 9 + i:10 + i] for i in range(2)]

        ids_sb = [sb(f"ids{i}", [GB, F], i32) for i in range(2)]
        rows_sb = [sb(f"rows{i}", [GB, F * D]) for i in range(2)]
        xh = [sb(f"xh{i}", [128, TK, CN]) for i in range(2)]
        xa = sb("xa", [JT * F, CN])
        xb = sb("xb", [JT * F, T0, CN])
        prod_whole = sb("prod_whole", [128, WHOLE_SLOTS, PAIR, CN])
        prod_pool = sb("prod_pool", [128, POOL_SLOTS, PAIR, CN])
        high = sb("high", [128, SPLIT_SLOTS, PAIR, CN], f32r)
        low = sb("low", [128, SPLIT_SLOTS, PAIR, CN], f32r)
        direct = sb("direct", [128, CN])
        last = sb("last", [128, CN])
        feats = sb("feats", [128, 2, B])

        stage_sb = xh[1][:, :, :].rearrange("p t n -> p (t n)")[:, 0:ALL_TILES * S].rearrange(
            "p (t s) -> p t s", s=S)
        flat = xh[0][:, :, :].rearrange("p t n -> p (t n)")
        n1, n2 = T1 // 128, T2 // 128
        wt1_sb = flat[:, 0:2 * T1].rearrange("p (i n) -> p i n", n=T1)
        wt2_sb = flat[:, 1024:1024 + n1 * T2].rearrange("p (i n) -> p i n", n=T2)
        wt1c_sb = flat[0:CTX, 2048:2048 + T1]
        ctx_sb = flat[0:CTX, 2560:2560 + B]
        h1 = xh[1][:, 0:n1, :]
        h2 = xh[1][:, n1:n1 + n2, :]
        y_sb = xh[1][0:1, 8:8 + B // MB, :]

        z = [bank(f"z{i}") for i in range(3)]
        xk = [bank("x1"), bank("x2")]
        xa_ps = bank("xa_ps")
        prod_dve = bank("prod_dve", PAIR)
        prod_dve_v = prod_dve[:, :].rearrange("p (i n) -> p i n", n=CN)
        mlp = [prod_dve[:, 0:512], prod_dve[:, 512:1024], xa_ps[:, :]]

        staged_loaded = sem("staged_loaded")
        cols_loaded = sem("cols_loaded")
        mlp_loaded = sem("mlp_loaded")
        w0_summed = sem("w0_summed")
        w_rounded = sem("w_rounded")
        w_ready = sem("w_ready")
        pads_cleared = sem("pads_cleared")
        ids_loaded = [sem(f"ids_loaded{i}") for i in range(2)]
        gather_begun = sem("gather_begun")
        gathered = [sem(f"gathered{i}") for i in range(2)]
        stored = [sem(f"stored{i}") for i in range(2)]
        xh_loaded = [sem(f"xh_loaded{i}") for i in range(2)]
        x0_loaded = sem("x0_loaded")
        xa_copied = sem("xa_copied")
        products_ready = sem("products_ready")
        high_ready = sem("high_ready")
        low_by_pool = sem("low_by_pool")
        low_by_dve = sem("low_by_dve")
        products_used = sem("products_used")
        relu_done = [sem(f"relu{i}_done") for i in range(3)]
        direct_summed = sem("direct_summed")
        last_summed = sem("last_summed")
        hidden1_done = sem("hidden1_done")
        hidden1_relu = sem("hidden1_relu")
        hidden2_done = sem("hidden2_done")
        hidden2_relu = sem("hidden2_relu")
        y_done = sem("y_done")
        y_copied = sem("y_copied")
        y_stored = sem("y_stored")

        def groups(stage, c):
            return PLAN[stage, c if isinstance(c, int) else LIKE + (stage == 0)]

        def count(c, group, value, per):
            if isinstance(c, int):
                return value
            return (c - group.chunk) * PER[per] + value

        def wait_count(engine, semaphore, c, group, value, per):
            if value > 0:
                engine.wait_ge(semaphore, count(c, group, value, per))

        def wait_made(engine, stage, c):
            group = groups(stage, c)[-1]
            wait_count(engine, products_ready, c, group, group.n + 1, "all")

        def over_chunks(engine, step):
            step(0, 0)
            step(1, 1)
            with engine.Fori(1, CHUNKS // 2 - 1) as i:
                step(2 * i, 0)
                step(2 * i + 1, 1)
            step(CHUNKS - 2, 0)
            step(CHUNKS - 1, 1)

        block = stack.enter_context(nc.Block())

        @block.sync
        def _(sp):
            def load_ids(t, p):
                sp.dma_start(ids_sb[p][:, :], ids[bass.ds(t * GB, GB), :]).then_inc(ids_loaded[p], 16)

            def store_rows(t, p, uses):
                sp.wait_ge(gathered[p], uses * F * 16)
                src = rows_sb[p][:, :].rearrange("b (f d) -> b f d", d=D)
                dst = x0_dram.rearrange("f (b d) -> b f d", d=D)[bass.ds(t * GB, GB), :, :]
                sp.dma_start(dst[:, 0:F, :], src).then_inc(stored[p], 16)
                sp.dma_start(dst[:, F:XROWS, :], src[:, 0:XROWS - F, :]).then_inc(stored[p], 16)

            def load_pairs(c):
                col = x0_dram[:, bass.ds(c * CN, CN)]
                for jj in range(JT):
                    n = (SHIFTS - jj + JT - 1) // JT
                    at = slice(jj * F, (jj + 1) * F)
                    sp.dma_start(xa[at, :], col[0:F, :]).then_inc(x0_loaded, 16)
                    step = col.ap[0][0]
                    shifted = bass.AP(tensor=col.tensor, offset=col.offset + jj * step,
                                      ap=[[step, F], [JT * step, n], [1, CN]])
                    sp.dma_start(xb[at, 0:n, :], shifted).then_inc(x0_loaded, 16)

            def load_fields(c, p):
                col = x0_dram[:, bass.ds(c * CN, CN)]
                step = col.ap[0][0]
                for hh in range(2):
                    n = (F + 1 - hh) // 2
                    spread = bass.AP(tensor=col.tensor, offset=col.offset + hh * step,
                                     ap=[[0, H], [2 * step, n], [1, CN]])
                    sp.dma_start(xh[p][hh * H:(hh + 1) * H, 0:n, :], spread).then_inc(xh_loaded[p], 16)

            def block_of_chunks(t, p, uses, first=False, next_ids=True, next_rows=True):
                sp.wait_ge(stored[p], uses * 32)
                for q in range(PER_GATHER):
                    c = PER_GATHER * t + q
                    if not (first and q == 0):
                        wait_made(sp, 0, c - 1)
                    load_pairs(c)
                    if not (first and q < 2):
                        wait_made(sp, 2, c - 2)
                    elif q == 1:
                        sp.wait_ge(pads_cleared, 2)
                    load_fields(c, q % 2)
                    if q == 0 and next_ids:
                        sp.wait_ge(gathered[p], uses * F * 16)
                        load_ids(t + 2, p)
                if next_rows:
                    store_rows(t + 1, 1 - p, uses if p == 0 else uses + 1)

            load_ids(0, 0)
            load_ids(1, 1)
            sp.dma_start(stage_sb, staged).then_inc(staged_loaded, 16)
            sp.dma_start(cols_sb[:, :], cols).then_inc(cols_loaded, 16)
            store_rows(0, 0, 1)
            block_of_chunks(0, 0, 1, first=True)
            block_of_chunks(1, 1, 1)
            with sp.Fori(1, GATHERS // 2 - 1) as i:
                block_of_chunks(2 * i, 0, i + 1)
                block_of_chunks(2 * i + 1, 1, i + 1)
            block_of_chunks(GATHERS - 2, 0, GATHERS // 2, next_ids=False)
            block_of_chunks(GATHERS - 1, 1, GATHERS // 2, next_ids=False, next_rows=False)
            wait_made(sp, 2, CHUNKS - 2)
            for dst, src in ((wt1_sb, wt1), (wt2_sb, wt2), (wt1c_sb, wt1c), (ctx_sb, ctx_t)):
                sp.dma_start(dst, src).then_inc(mlp_loaded, 16)
            sp.wait_ge(y_copied, B // MB)
            sp.dma_start(out.rearrange("(m b) o -> o m b", b=MB), y_sb).then_inc(y_stored, 16)
            sp.wait_ge(y_stored, 16)

        @block.gpsimd
        def _(pool):
            def begin_gather(p, uses, first=False):
                pool.wait_ge(ids_loaded[p], uses * 16)
                if not first:
                    pool.wait_ge(stored[p], (uses - 1) * 32)
                pool.sem_inc(gather_begun, 1)

            def gather(p, f):
                pool.indirect_dma_start(
                    rows_sb[p][:, f * D:(f + 1) * D], None, tables[f],
                    bass.IndirectOffsetOnAxis(ap=ids_sb[p][:, f:f + 1], axis=0),
                ).then_inc(gathered[p], 16)

            def chunk(c, p=None, fields=()):
                fields = list(fields)
                stages = [(1, c), (0, c + 1), (2, c)]
                if isinstance(c, int) and c == CHUNKS - 1:
                    stages.pop(1)
                mine = [(g, at) for s, at in stages for g in groups(s, at) if g.kind == BY_POOL]
                for i, (g, at) in enumerate(mine):
                    low_parts(g, at)
                    share = -(-len(fields) // (len(mine) - i))
                    for _ in range(share):
                        gather(p, fields.pop(0))

            def low_parts(g, c):
                wait_count(pool, high_ready, c, g, g.k + 1, "split")
                n = len(g.tiles)
                pool.tensor_tensor(
                    low[0:g.rows, g.split_slot, 0:n, :], prod_pool[0:g.rows, g.slot, 0:n, :],
                    high[0:g.rows, g.split_slot, 0:n, :].bitcast(f32), ALU.subtract,
                ).then_inc(low_by_pool, 1)

            pool.memset(xh[0][H:128, TK - 1, :], 0.0).then_inc(pads_cleared, 1)
            begin_gather(0, 1, True)
            for f in range(F):
                gather(0, f)
            pool.wait_ge(w_ready, 1)
            pool.memset(xh[1][H:128, TK - 1, :], 0.0).then_inc(pads_cleared, 1)
            pool.wait_ge(pads_cleared, 2)
            begin_gather(1, 1, True)
            for g in groups(0, 0):
                if g.kind == BY_POOL:
                    low_parts(g, 0)
            half = (F + 1) // 2
            chunk(0, 1, range(half))
            chunk(1, 1, range(half, F))

            quarters = [range(F * q // PER_GATHER, F * (q + 1) // PER_GATHER) for q in range(PER_GATHER)]
            with pool.Fori(0, GATHERS // 2 - 1) as i:
                for p in range(2):
                    begin_gather(p, i + 2)
                    for q in range(PER_GATHER):
                        chunk(i * (2 * PER_GATHER) + (2 + PER_GATHER * p + q), p, quarters[q])
            for c in range(2 + PER_GATHER * (GATHERS - 2), CHUNKS):
                chunk(c)

        @block.vector
        def _(dve):
            def low_parts(g, c):
                wait_count(dve, high_ready, c, g, g.k + 1, "split")
                n = len(g.tiles)
                dve.tensor_tensor(
                    low[0:g.rows, g.split_slot, 0:n, :], prod_dve_v[0:g.rows, 0:n, :],
                    high[0:g.rows, g.split_slot, 0:n, :].bitcast(f32), ALU.subtract,
                ).then_inc(low_by_dve, 1)

            def products(stage, c, spread, shared, after=None):
                owed = None
                for g in groups(stage, c):
                    if g.kind == WHOLE:
                        into = prod_whole[:, g.slot, :, :]
                        if g.of_kind >= WHOLE_SLOTS:
                            wait_count(dve, products_used, c, g,
                                       WHOLES[g.of_kind - WHOLE_SLOTS].n + 1, "all")
                    elif g.kind == BY_POOL:
                        into = prod_pool[:, g.slot, :, :]
                        wait_count(dve, low_by_pool, c, g, g.of_kind - POOL_SLOTS + 1, BY_POOL)
                    else:
                        into = prod_dve_v
                        wait_count(dve, low_by_dve, c, g, g.of_kind, BY_DVE)
                    n = len(g.tiles)
                    t = slice(g.tiles[0], g.tiles[0] + n)
                    dve.tensor_tensor(
                        into[0:g.rows, 0:n, :], spread[0:g.rows, t, :],
                        shared[0:g.rows, :].unsqueeze(1).broadcast_to([g.rows, n, CN]), ALU.mult,
                    ).then_inc(products_ready, 1)
                    if owed:
                        low_parts(owed, c)
                    owed = g if g.kind == BY_DVE else None
                    if g.g == AFTER and after:
                        after()
                assert not owed

            def sum_over_d(into, src, done):
                dve.tensor_reduce(into, src[:, :].rearrange("p (b d) -> p b d", d=D),
                                  axis=AX.X, op=ALU.add).then_inc(done, 1)

            def sum_last(c):
                dve.wait_ge(relu_done[2], c + 1)
                sum_over_d(feats[:, 1, bass.ds(c * CB, CB)], last, last_summed)

            def sum_direct(c):
                dve.wait_ge(relu_done[1], 3 * c + 3)
                sum_over_d(feats[:, 0, bass.ds(c * CB, CB)], direct, direct_summed)

            def layer0(c):
                dve.wait_ge(x0_loaded, (c + 1) * 2 * JT * 16)
                dve.wait_ge(xa_copied, c + 1)
                products(0, c, xb, xa_ps)

            def chunk(c, p):
                dve.wait_ge(xh_loaded[p], 16 * (c - p) + 32)
                dve.wait_ge(relu_done[0], 3 * c + 2)
                begun = isinstance(c, int) and c == 0
                products(1, c, xh[p], xk[0], None if begun else lambda: sum_last(c - 1))
                if not (isinstance(c, int) and c == CHUNKS - 1):
                    layer0(c + 1)
                dve.wait_ge(relu_done[1], 3 * c + 2)
                products(2, c, xh[p], xk[1], lambda: sum_direct(c))

            dve.wait_ge(staged_loaded, 16)
            dve.tensor_tensor(stage_sb[:, 0:T0, :], stage_sb[:, 0:T0, :],
                              stage_sb[:, TURNED:TURNED + T0, :], ALU.add).then_inc(w0_summed, 1)
            dve.wait_ge(w0_summed, 1)
            firsts = [g for stage in range(3) for g in PLAN[stage, 0]]

            def weight_tiles(g):
                n = len(g.tiles)
                to = (SPLIT_TILE if g.split else WHOLE_TILE)[g.stage, g.tiles[0]]
                at = STAGED[g.stage] + g.tiles[0]
                return slice(to, to + n), stage_sb[:, at:at + n, :]

            for g in firsts:
                to, src = weight_tiles(g)
                dve.tensor_copy((w_high if g.split else w_whole)[:, to, :], src).then_inc(w_rounded, 1)
            dve.wait_ge(w_rounded, len(firsts))
            for g in firsts:
                if g.split:
                    to, src = weight_tiles(g)
                    last_low = dve.tensor_tensor(w_low[:, to, :], src, w_high[:, to, :].bitcast(f32),
                                                 ALU.subtract)
            last_low.then_inc(w_ready, 1)
            dve.wait_ge(pads_cleared, 1)
            layer0(0)
            over_chunks(dve, chunk)
            sum_last(CHUNKS - 1)
            for m in range(B // MB):
                dve.wait_ge(y_done, m + 1)
                dve.tensor_copy(y_sb[:, m, :], mlp[2][0:1, :]).then_inc(y_copied, 1)

        @block.tensor
        def _(pe):
            def contract(stage, c):
                if not (isinstance(c, int) and c == 0):
                    pe.wait_ge(relu_done[stage], (1 if stage == 2 else 3) * c)
                for g in groups(stage, c):
                    def mm(weights, table, src, i, is_last=False):
                        t = g.tiles[i]
                        return pe.matmul(
                            z[stage][:, :], weights[0:g.rows, table[stage, t], :],
                            src[0:g.rows, i, :], start=t == 0 and weights is not w_low and src is not lows,
                            stop=g.ends_layer and is_last)

                    every = range(len(g.tiles))
                    lows = None
                    if g.kind == WHOLE:
                        wait_count(pe, products_ready, c, g, g.n + 1, "all")
                        src = prod_whole[:, g.slot, :, :]
                        for i in every:
                            done = mm(w_whole, WHOLE_TILE, src, i, i == every[-1])
                    else:
                        wait_count(pe, high_ready, c, g, g.k + 1, "split")
                        highs = high[:, g.split_slot, :, :]
                        lows = low[:, g.split_slot, :, :]
                        for i in every:
                            mm(w_high, SPLIT_TILE, highs, i)
                            mm(w_low, SPLIT_TILE, highs, i)
                        made = low_by_pool if g.kind == BY_POOL else low_by_dve
                        wait_count(pe, made, c, g, g.of_kind + 1, g.kind)
                        for i in every:
                            done = mm(w_high, SPLIT_TILE, lows, i, i == every[-1])
                    done.then_inc(products_used, 1)

            def chunk(c, p):
                contract(1, c)
                if not (isinstance(c, int) and c == CHUNKS - 1):
                    contract(0, c + 1)
                contract(2, c)

            pe.wait_ge(w_ready, 1)
            contract(0, 0)
            over_chunks(pe, chunk)

            pe.wait_ge(mlp_loaded, 64)
            pe.wait_ge(cols_loaded, 16)
            pe.wait_ge(direct_summed, CHUNKS)
            pe.wait_ge(last_summed, CHUNKS)
            for m in range(B // MB):
                at = slice(m * MB, (m + 1) * MB)
                for j in range(n1):
                    k = n1 * m + j
                    if k >= 2:
                        pe.wait_ge(hidden1_relu, k - 1)
                    if m and j < 2:
                        pe.wait_ge(hidden2_relu, n2 * m - 1 + j)
                    js = slice(j * 128, (j + 1) * 128)
                    acc = mlp[k % 2]
                    pe.matmul(acc, wt1_sb[:, 0, js], feats[:, 0, at], start=True, stop=False)
                    pe.matmul(acc, wt1_sb[:, 1, js], feats[:, 1, at], start=False, stop=False)
                    pe.matmul(acc, wt1c_sb[:, js], ctx_sb[:, at], start=False,
                              stop=True).then_inc(hidden1_done, 1)
                pe.wait_ge(hidden1_relu, n1 * (m + 1))
                for j in range(n2):
                    js = slice(j * 128, (j + 1) * 128)
                    for i in range(n1):
                        mm = pe.matmul(mlp[j], wt2_sb[:, i, js], h1[:, i, :],
                                       start=i == 0, stop=i == n1 - 1)
                    mm.then_inc(hidden2_done, 1)
                pe.wait_ge(hidden2_relu, n2 * (m + 1))
                if m:
                    pe.wait_ge(y_copied, m)
                for i in range(n2):
                    mm = pe.matmul(mlp[2][0:1, :], wt3[i], h2[:, i, :], start=i == 0, stop=i == n2 - 1)
                mm.then_inc(y_done, 1)

        @block.scalar
        def _(act):
            def layer_out(stage, c):
                end = groups(stage, c)[-1]
                wait_count(act, products_used, c, end, end.n + 1, "all")
                begun = isinstance(c, int) and c == 0
                if stage == 2:
                    if not begun:
                        act.wait_ge(last_summed, c)
                    act.activation(last[:, :], z[2][:, :], ACT.Relu,
                                   bias=bias[2]).then_inc(relu_done[2], 1)
                    return
                if not begun:
                    wait_made(act, stage + 1, c - 1)
                feed = slice(0, H) if stage == 0 else slice(H, 128)
                leave = slice(H, 128) if stage == 0 else slice(0, H)
                for half in (slice(0, H), slice(H, 128)):
                    act.activation(xk[stage][half, :], z[stage][feed, :], ACT.Relu,
                                   bias=bias[stage][feed, :]).then_inc(relu_done[stage], 1)
                if stage == 0 and not begun:
                    act.wait_ge(direct_summed, c)
                act.activation(direct[leave, :], z[stage][leave, :], ACT.Relu,
                               bias=bias[stage][leave, :]).then_inc(relu_done[stage], 1)

            def copy_xa(c):
                act.wait_ge(x0_loaded, (c + 1) * 2 * JT * 16)
                if not (isinstance(c, int) and c == 0):
                    wait_made(act, 0, c - 1)
                act.activation(xa_ps[0:JT * F, :], xa[:, :], ACT.Copy).then_inc(xa_copied, 1)

            def round_group(g, c):
                wait_count(act, products_ready, c, g, g.n + 1, "all")
                if g.k >= SPLIT_SLOTS:
                    wait_count(act, products_used, c, g, SPLITS[g.k - SPLIT_SLOTS].n + 1, "all")
                n = len(g.tiles)
                src = prod_pool[:, g.slot, :, :] if g.kind == BY_POOL else prod_dve_v
                act.activation(high[0:g.rows, g.split_slot, 0:n, :], src[0:g.rows, 0:n, :],
                               ACT.Copy).then_inc(high_ready, 1)

            def round_stage(stage, c, between=()):
                between = dict(between)
                for i, g in enumerate(g for g in groups(stage, c) if g.split):
                    round_group(g, c)
                    if i in between:
                        between[i]()

            def chunk(c, p):
                final = isinstance(c, int) and c == CHUNKS - 1
                begun = isinstance(c, int) and c == 0
                during1 = {}
                if not begun:
                    during1[OUT2] = lambda: layer_out(2, c - 1)
                if not final:
                    during1[XA] = lambda: copy_xa(c + 1)
                round_stage(1, c, during1)
                if not final:
                    round_stage(0, c + 1)
                layer_out(1, c)
                round_stage(2, c, {} if final else {OUT0: lambda: layer_out(0, c + 1)})

            act.wait_ge(cols_loaded, 16)
            copy_xa(0)
            round_stage(0, 0)
            layer_out(0, 0)
            over_chunks(act, chunk)
            layer_out(2, CHUNKS - 1)

            for m in range(B // MB):
                for j in range(n1):
                    k = n1 * m + j
                    act.wait_ge(hidden1_done, k + 1)
                    if m and j == 0:
                        act.wait_ge(hidden2_done, n2 * m)
                    act.activation(h1[:, j, :], mlp[k % 2], ACT.Relu,
                                   bias=bt1[j]).then_inc(hidden1_relu, 1)
                for j in range(n2):
                    act.wait_ge(hidden2_done, n2 * m + j + 1)
                    if m and j == 0:
                        act.wait_ge(y_done, m)
                    act.activation(h2[:, j, :], mlp[j], ACT.Relu,
                                   bias=bt2[j]).then_inc(hidden2_relu, 1)


def kernel(**inputs):
    import concourse.bacc as bacc
    from concourse.bass_utils import run_bass_kernel_spmd

    a = {k: np.ascontiguousarray(np.asarray(v)) for k, v in inputs.items()}

    w0 = a["L0_rec_w0"]
    w0a = np.zeros((128, T0, S), w0.dtype)
    w0b = np.zeros((128, T0, S), w0.dtype)
    first = np.arange(F)
    for j in range(SHIFTS):
        second = (first + j) % F
        at = slice(j % JT * F, (j % JT + 1) * F)
        w0a[at, j // JT] = w0[first, second]
        if j:
            w0b[at, j // JT] = w0[second, first]

    def by_fields(w):
        tiles = np.zeros((2 * TK, H, w.shape[2]), w.dtype)
        tiles[:F] = w
        return np.ascontiguousarray(tiles.reshape(TK, 2 * H, w.shape[2]).transpose(1, 0, 2))

    def by_128(m):
        return np.ascontiguousarray(m.reshape(-1, 128, m.shape[1]).transpose(1, 0, 2))

    turned = np.r_[H:S, 0:H]
    wt1 = a["W_top1"]
    cols = np.concatenate(
        [a["L0_rec_b0"].reshape(1, S), a["L0_rec_b1"][turned].reshape(1, S),
         a["L0_rec_b2"].reshape(1, S), a["b_top1"].reshape(-1, 128), a["b_top2"].reshape(-1, 128),
         a["W_top3"].reshape(-1, 128)]).T
    arrays = {
        "ids": a["ids"],
        "ctx_t": np.ascontiguousarray(a["dense_ctx"].T),
        "staged": np.concatenate([w0a, by_fields(a["L0_rec_w1"][:, :, turned]),
                                  by_fields(a["L0_rec_w2"]), w0b], axis=1),
        "wt1": by_128(np.concatenate([wt1[H:2 * H], wt1[0:H], wt1[2 * H:4 * H]])),
        "wt1c": np.ascontiguousarray(wt1[4 * H:]),
        "wt2": by_128(a["W_top2"]),
        "cols": np.ascontiguousarray(cols),
    }
    names = list(arrays)
    for f in range(F):
        arrays[f"tbl_{f}"] = a[f"tbl_{f}"]

    nc = bacc.Bacc("TRN2", target_bir_lowering=False, num_devices=1)
    dram = {k: nc.dram_tensor(k, v.shape, mybir.dt.from_np(v.dtype), kind="ExternalInput").ap()
            for k, v in arrays.items()}
    out = nc.dram_tensor("out", (B, 1), mybir.dt.float32, kind="ExternalOutput").ap()
    tower(nc, [dram[f"tbl_{f}"] for f in range(F)], *[dram[k] for k in names], out)
    r = run_bass_kernel_spmd(nc, [arrays], core_ids=[0])
    return r.results[0]["out"]
```

```python
from contextlib import ExitStack

import concourse.bass as bass
import concourse.mybir as mybir
import numpy as np

B, F, D = 2048, 39, 16
S, H = 128, 64
N = B * D
CB = 32
CN = CB * D
CHUNKS = B // CB

FG = 128 // CB
GATHERS = -(-F // FG)
LAST_FG = F - (FG - 1) * GATHERS

SHIFTS = (F + 1) // 2
JT = 3
T0 = -(-SHIFTS // JT)
LAST0 = (SHIFTS - JT * (T0 - 1)) * F
XROWS = F + SHIFTS - 1
TK = -(-F // 2)

PAIR = 2
G0, GK = -(-T0 // PAIR), TK // PAIR
STORES = -(-F // GATHERS) + -(-(XROWS - F) // GATHERS)
WHOLE, BY_POOL, BY_DVE = "whole", "low parts by GpSimd", "low parts by VectorE"
KINDS = {
    0: [BY_POOL, BY_DVE, BY_POOL, WHOLE],
    1: [WHOLE, BY_POOL, WHOLE, BY_DVE, BY_POOL, WHOLE, BY_POOL, BY_DVE, BY_POOL, WHOLE],
}
KINDS[2] = KINDS[1]
WHOLE_SLOTS, POOL_SLOTS, SPLIT_SLOTS = 3, 2, 5

SUM_AFTER, LAST_OUT_AFTER, XA_AFTER, FIRST_OUT_AFTER = 9, 5, 4, 5
T1, T2 = 512, 256
CTX = 16
MB = 512
MSTEPS = B // MB

STAGED = {0: 0, 1: T0, 2: T0 + TK}
TURNED = T0 + 2 * TK
ALL_TILES = TURNED + T0


class Group:

    def __init__(self, stage, chunk, g, counts):
        total = T0 if stage == 0 else TK
        self.stage, self.chunk, self.g, self.kind = stage, chunk, g, KINDS[stage][g]
        self.tiles = range(PAIR * g, min(PAIR * (g + 1), total))
        self.ends_layer = self.tiles[-1] == total - 1
        self.rows = 128 if stage else (LAST0 if self.ends_layer else JT * F)
        self.split = self.kind != WHOLE
        self.n = counts["all"]
        self.k = counts["split"]
        self.of_kind = counts[self.kind]
        counts["all"] += 1
        counts["split"] += self.split
        counts[self.kind] += 1
        self.slot = self.of_kind % {WHOLE: WHOLE_SLOTS, BY_POOL: POOL_SLOTS, BY_DVE: 1}[self.kind]
        self.split_slot = self.k % SPLIT_SLOTS


def plan():
    counts = dict.fromkeys(("all", "split", WHOLE, BY_POOL, BY_DVE), 0)
    order = [(0, 0)]
    for c in range(CHUNKS):
        order += [(1, c)] + [(0, c + 1)] * (c + 1 < CHUNKS) + [(2, c)]
    return {(stage, c): [Group(stage, c, g, counts) for g in range(len(KINDS[stage]))]
            for stage, c in order}


PLAN = plan()
EVERY = [g for gs in PLAN.values() for g in gs]
SPLITS = [g for g in EVERY if g.split]
WHOLES = [g for g in EVERY if not g.split]
LIKE = 2
PER = {"all": sum(map(len, KINDS.values())),
       "split": sum(k != WHOLE for ks in KINDS.values() for k in ks),
       BY_POOL: sum(k == BY_POOL for ks in KINDS.values() for k in ks),
       BY_DVE: sum(k == BY_DVE for ks in KINDS.values() for k in ks)}
assert (PER["all"] - PER["split"]) % WHOLE_SLOTS == 0
assert PER[BY_POOL] % POOL_SLOTS == 0 and PER["split"] % SPLIT_SLOTS == 0

WHOLE_TILE, SPLIT_TILE = {}, {}
for _stage in range(3):
    for _group in PLAN[_stage, 0]:
        for _t in _group.tiles:
            _to = SPLIT_TILE if _group.split else WHOLE_TILE
            _to[_stage, _t] = len(_to)


def tower(nc, table, ids, row_base, ctx_t, staged, wt1, wt1c, wt2, cols, out):
    f32, f32r, i32 = mybir.dt.float32, mybir.dt.float32r, mybir.dt.int32
    ALU, ACT, AX = mybir.AluOpType, mybir.ActivationFunctionType, mybir.AxisListType

    x0_dram = nc.dram_tensor("x0_rows", (XROWS, N), f32, kind="Internal").ap()
    feats_dram = nc.dram_tensor("feats_all", (128, 2, B), f32, kind="Internal").ap()

    with ExitStack() as stack:
        def sb(name, shape, dt=f32):
            return stack.enter_context(nc.sbuf_tensor(name, shape, dt))

        def bank(name, banks=1):
            return stack.enter_context(nc.psum_tensor(name, [128, banks * 512], f32))

        def sem(name):
            return stack.enter_context(nc.semaphore(name))

        w_whole = sb("w_whole", [128, len(WHOLE_TILE), S])
        w_high = sb("w_high", [128, len(SPLIT_TILE), S], f32r)
        w_low = sb("w_low", [128, len(SPLIT_TILE), S], f32r)
        cols_sb = sb("cols_sb", [128, 3 + T1 // 128 + 2 * (T2 // 128)])
        bias = [cols_sb[:, i:i + 1] for i in range(3)]
        bt1 = [cols_sb[:, 3 + i:4 + i] for i in range(4)]
        bt2 = [cols_sb[:, 7 + i:8 + i] for i in range(2)]
        wt3 = [cols_sb[:, 9 + i:10 + i] for i in range(2)]

        row_base_sb = sb("row_base_sb", [128, GATHERS], i32)
        ids_sb = [sb(f"ids{i}", [128, GATHERS], i32) for i in range(2)]
        index = [sb(f"index{i}", [128, GATHERS], i32) for i in range(2)]
        rows_sb = [sb(f"rows{i}", [128, GATHERS * D]) for i in range(2)]
        xh = [sb(f"xh{i}", [128, TK, CN]) for i in range(2)]
        xa = sb("xa", [JT * F, CN])
        xb = sb("xb", [JT * F, T0, CN])
        prod_whole = sb("prod_whole", [128, WHOLE_SLOTS, PAIR, CN])
        prod_pool = sb("prod_pool", [128, POOL_SLOTS, PAIR, CN])
        high = sb("high", [128, SPLIT_SLOTS, PAIR, CN], f32r)
        low = sb("low", [128, SPLIT_SLOTS, PAIR, CN], f32r)
        direct = sb("direct", [128, CN])
        last = sb("last", [128, CN])
        chunk_feats = [sb(f"chunk_feats{i}", [128, 2, CB]) for i in range(2)]

        stage_sb = xh[1][:, :, :].rearrange("p t n -> p (t n)")[:, 0:ALL_TILES * S].rearrange(
            "p (t s) -> p t s", s=S)
        flat = xh[0][:, :, :].rearrange("p t n -> p (t n)")
        n1, n2 = T1 // 128, T2 // 128
        wt1_sb = flat[:, 0:2 * T1].rearrange("p (i n) -> p i n", n=T1)
        wt2_sb = flat[:, 1024:1024 + n1 * T2].rearrange("p (i n) -> p i n", n=T2)
        wt1c_sb = flat[0:CTX, 2048:2048 + T1]
        ctx_sb = flat[0:CTX, 2560:2560 + B]
        feats = flat[:, 4608:4608 + 2 * B].rearrange("p (i b) -> p i b", b=B)
        h1 = xh[1][:, 0:n1, :]
        h2 = xh[1][:, n1:n1 + n2, :]
        y_sb = xh[1][0:1, 8:8 + MSTEPS, :]

        mlp_weights = [("wt1", wt1_sb), ("wt1c", wt1c_sb), ("wt2", wt2_sb)]
        FIRST_LAYER = 2

        def mlp_inputs(m):
            at = slice(m * MB, (m + 1) * MB)
            return [("feats", feats[:, :, at]), ("ctx", ctx_sb[:, at])]

        def split_places(weights, products):
            w = weights[:, :, :].rearrange("p t s -> p (t s)")
            x = products[:, :, :, :].rearrange("p s i n -> p (s i) n")
            return {"wt1": w[:, 0:2 * T1].rearrange("p (i n) -> p i n", n=T1),
                    "wt1c": w[0:CTX, 2 * T1:3 * T1],
                    "wt2": w[:, 3 * T1:3 * T1 + n1 * T2].rearrange("p (i n) -> p i n", n=T2),
                    "feats": [x[:, 0:2, :], x[:, 3:5, :]],
                    "ctx": [x[0:CTX, 2, :], x[0:CTX, 5, :]],
                    "h1": x[:, 6:6 + n1, :]}

        assert 3 * T1 <= S * sum(stage < 2 for stage, _ in SPLIT_TILE)
        hi, lo = split_places(w_high, high), split_places(w_low, low)
        wt2_end = -(-(3 * T1 + n1 * T2) // S)
        WT2_FREE = 1 + max(g.n for g in PLAN[2, CHUNKS - 1]
                           if g.split and SPLIT_TILE[2, g.tiles[0]] < wt2_end)
        INPUTS_FREE = 1 + max(g.n for g in SPLITS if g.split_slot < 2)

        z = [bank(f"z{i}") for i in range(3)]
        xk = [bank("x1"), bank("x2")]
        xa_ps = bank("xa_ps")
        prod_dve = bank("prod_dve", PAIR)
        prod_dve_v = prod_dve[:, :].rearrange("p (i n) -> p i n", n=CN)
        z_h1 = [prod_dve[:, 0:512], prod_dve[:, 512:1024], xk[0][:, :], xk[1][:, :]]
        z_h2 = [z[0][:, :], z[1][:, :]]
        z_y = z[2][0:1, :]

        staged_loaded = [sem(f"staged{i}_loaded") for i in range(3)]
        cols_loaded = sem("cols_loaded")
        mlp_loaded = sem("mlp_loaded")
        w0_summed = sem("w0_summed")
        w_rounded = sem("w_rounded")
        w_ready = sem("w_ready")
        pads_cleared = sem("pads_cleared")
        ids_loaded = [sem(f"ids_loaded{i}") for i in range(2)]
        base_loaded = sem("base_loaded")
        index_ready = sem("index_ready")
        gather_begun = sem("gather_begun")
        gathered = [sem(f"gathered{i}") for i in range(2)]
        stored = [sem(f"stored{i}") for i in range(2)]
        xh_loaded = [sem(f"xh_loaded{i}") for i in range(2)]
        x0_loaded = sem("x0_loaded")
        xa_copied = sem("xa_copied")
        products_ready = sem("products_ready")
        high_ready = sem("high_ready")
        low_by_pool = sem("low_by_pool")
        low_by_dve = sem("low_by_dve")
        products_used = sem("products_used")
        relu_done = [sem(f"relu{i}_done") for i in range(3)]
        direct_summed = sem("direct_summed")
        feats_stored = [sem(f"feats_stored{i}") for i in range(2)]
        feats_loaded = [sem(f"feats_loaded{i}") for i in range(MSTEPS)]
        last_summed = sem("last_summed")
        mlp_high = sem("mlp_high")
        mlp_low = sem("mlp_low")
        inputs_high = sem("inputs_high")
        inputs_low = sem("inputs_low")
        hidden1_done = sem("hidden1_done")
        hidden1_relu = sem("hidden1_relu")
        hidden1_high = sem("hidden1_high")
        hidden1_low = sem("hidden1_low")
        hidden2_done = sem("hidden2_done")
        hidden2_relu = sem("hidden2_relu")
        y_done = sem("y_done")
        y_copied = sem("y_copied")
        y_stored = sem("y_stored")

        def groups(stage, c):
            return PLAN[stage, c if isinstance(c, int) else LIKE + (stage == 0)]

        def count(c, group, value, per):
            if isinstance(c, int):
                return value
            return (c - group.chunk) * PER[per] + value

        def wait_count(engine, semaphore, c, group, value, per):
            if value > 0:
                engine.wait_ge(semaphore, count(c, group, value, per))

        def wait_made(engine, stage, c):
            group = groups(stage, c)[-1]
            wait_count(engine, products_ready, c, group, group.n + 1, "all")

        def over_chunks(engine, step, tail=2):
            step(0, 0)
            step(1, 1)
            with engine.Fori(1, (CHUNKS - tail) // 2) as i:
                step(2 * i, 0)
                step(2 * i + 1, 1)
            for c in range(CHUNKS - tail, CHUNKS):
                step(c, c % 2)

        firsts = [g for stage in range(3) for g in PLAN[stage, 0]]
        N_GROUPS, N_SPLIT = len(firsts), sum(g.split for g in firsts)

        def weight_tiles(g):
            n = len(g.tiles)
            to = (SPLIT_TILE if g.split else WHOLE_TILE)[g.stage, g.tiles[0]]
            at = STAGED[g.stage] + g.tiles[0]
            return slice(to, to + n), stage_sb[:, at:at + n, :]

        block = stack.enter_context(nc.Block())

        @block.sync
        def _(sp):
            def load_ids(c, p):
                sp.dma_start(ids_sb[p][:, :], ids[bass.ds(c * 128, 128), :]).then_inc(ids_loaded[p], 16)

            def store_rows(c, p):
                sp.wait_ge(gathered[p], 8 * GATHERS * (c - p) + 16 * GATHERS)
                col = x0_dram[:, bass.ds(c * CN, CN)]
                for again in range(2):
                    for g in range(FG):
                        f0 = g * GATHERS
                        n = min(GATHERS, (XROWS - F if again else F) - f0)
                        if n > 0:
                            src = rows_sb[p][g * CB:(g + 1) * CB, 0:n * D]
                            dst = col[again * F + f0:again * F + f0 + n, :]
                            sp.dma_start(dst.rearrange("f (b d) -> b f d", d=D),
                                         src.rearrange("b (f d) -> b f d", d=D)
                                         ).then_inc(stored[p], 16)

            def load_pairs(c):
                col = x0_dram[:, bass.ds(c * CN, CN)]
                for jj in range(JT):
                    n = (SHIFTS - jj + JT - 1) // JT
                    at = slice(jj * F, (jj + 1) * F)
                    sp.dma_start(xa[at, :], col[0:F, :]).then_inc(x0_loaded, 16)
                    step = col.ap[0][0]
                    shifted = bass.AP(tensor=col.tensor, offset=col.offset + jj * step,
                                      ap=[[step, F], [JT * step, n], [1, CN]])
                    sp.dma_start(xb[at, 0:n, :], shifted).then_inc(x0_loaded, 16)

            def load_fields(c, p):
                col = x0_dram[:, bass.ds(c * CN, CN)]
                step = col.ap[0][0]
                for hh in range(2):
                    n = (F + 1 - hh) // 2
                    spread = bass.AP(tensor=col.tensor, offset=col.offset + hh * step,
                                     ap=[[0, H], [2 * step, n], [1, CN]])
                    sp.dma_start(xh[p][hh * H:(hh + 1) * H, 0:n, :], spread).then_inc(xh_loaded[p], 16)

            def store_feats(c, p):
                sp.wait_ge(direct_summed, c + 1)
                sp.wait_ge(last_summed, c + 1)
                sp.dma_start(feats_dram[:, :, bass.ds(c * CB, CB)],
                             chunk_feats[p][:, :, :]).then_inc(feats_stored[p], 16)

            def chunk(c, p):
                known = isinstance(c, int)
                store_rows(c, p)
                if not known or c + 2 < CHUNKS:
                    sp.wait_ge(index_ready, c + 1)
                    load_ids(c + 2, p)
                sp.wait_ge(stored[p], 8 * STORES * (c - p) + 16 * STORES)
                if not known or c >= 1:
                    wait_made(sp, 0, c - 1)
                load_pairs(c)
                if not known or c >= 2:
                    wait_made(sp, 2, c - 2)
                elif c == 1:
                    sp.wait_ge(pads_cleared, 2)
                load_fields(c, p)
                if not known or c >= 2:
                    store_feats(c - 2, p)

            load_ids(0, 0)
            sp.dma_start(row_base_sb[:, :], row_base).then_inc(base_loaded, 16)
            load_ids(1, 1)
            for i, (at, n) in enumerate([(0, T0), (TURNED, T0), (T0, TK), (T0 + TK, TK)]):
                sp.dma_start(stage_sb[:, at:at + n, :], staged[:, at:at + n, :]
                             ).then_inc(staged_loaded[max(i - 1, 0)], 16)
            sp.dma_start(cols_sb[:, :], cols).then_inc(cols_loaded, 16)
            over_chunks(sp, chunk)
            wait_made(sp, 2, CHUNKS - 2)
            for dst, src in ((wt1_sb, wt1), (wt2_sb, wt2), (wt1c_sb, wt1c), (ctx_sb, ctx_t)):
                sp.dma_start(dst, src).then_inc(mlp_loaded, 16)
            for m in range(MSTEPS):
                if m == MSTEPS - 1:
                    for c in range(CHUNKS - 2, CHUNKS):
                        store_feats(c, c % 2)
                for p in range(2):
                    sp.wait_ge(feats_stored[p], 16 * (m + 1) * (MB // CB) // 2)
                at = slice(m * MB, (m + 1) * MB)
                sp.dma_start(feats[:, :, at], feats_dram[:, :, at]).then_inc(feats_loaded[m], 16)
            sp.wait_ge(y_copied, MSTEPS)
            sp.dma_start(out.rearrange("(m b) o -> o m b", b=MB), y_sb).then_inc(y_stored, 16)
            sp.wait_ge(y_stored, 16)

        @block.gpsimd
        def _(pool):
            def begin_gather(c, p):
                pool.wait_ge(ids_loaded[p], 8 * (c - p) + 16)
                pool.tensor_tensor(index[p][:, :], ids_sb[p][:, :], row_base_sb[:, :],
                                   ALU.add).then_inc(index_ready, 1)
                if not isinstance(c, int) or c >= 2:
                    pool.wait_ge(stored[p], 8 * STORES * (c - p))
                pool.wait_ge(index_ready, c + 1)
                pool.sem_inc(gather_begun, 1)

            def gather(p, j):
                n = CB * (FG if j < LAST_FG else FG - 1)
                pool.indirect_dma_start(
                    rows_sb[p][0:n, j * D:(j + 1) * D], None, table,
                    bass.IndirectOffsetOnAxis(ap=index[p][0:n, j:j + 1], axis=0),
                ).then_inc(gathered[p], 16)

            def chunk(c, p):
                known = isinstance(c, int)
                gathers = [(c + 3, 1 - p)] if not known or c + 3 < CHUNKS else []
                if known and c == 0:
                    gathers.insert(0, (2, 0))
                left = [(at, q, j) for at, q in gathers for j in range(GATHERS)]
                stages = [(1, c), (0, c + 1), (2, c)]
                if known and c == CHUNKS - 1:
                    stages.pop(1)
                mine = [(g, at) for s, at in stages for g in groups(s, at) if g.kind == BY_POOL]
                for i, (g, at) in enumerate(mine):
                    low_parts(g, at)
                    for _ in range(-(-len(left) // (len(mine) - i))):
                        at, q, j = left.pop(0)
                        if j == 0:
                            begin_gather(at, q)
                        gather(q, j)

            def low_parts(g, c):
                wait_count(pool, high_ready, c, g, g.k + 1, "split")
                n = len(g.tiles)
                pool.tensor_tensor(
                    low[0:g.rows, g.split_slot, 0:n, :], prod_pool[0:g.rows, g.slot, 0:n, :],
                    high[0:g.rows, g.split_slot, 0:n, :].bitcast(f32), ALU.subtract,
                ).then_inc(low_by_pool, 1)

            pool.memset(xh[0][H:128, TK - 1, :], 0.0).then_inc(pads_cleared, 1)
            pool.wait_ge(pads_cleared, 1)
            pool.wait_ge(base_loaded, 16)
            for c in range(2):
                begin_gather(c, c)
                for j in range(GATHERS):
                    gather(c, j)
            pool.wait_ge(w_ready, N_SPLIT)
            pool.wait_ge(w_rounded, N_GROUPS)
            pool.memset(xh[1][H:128, TK - 1, :], 0.0).then_inc(pads_cleared, 1)
            pool.wait_ge(pads_cleared, 2)
            for g in groups(0, 0):
                if g.kind == BY_POOL:
                    low_parts(g, 0)
            over_chunks(pool, chunk, tail=4)

        @block.vector
        def _(dve):
            def low_parts(g, c):
                wait_count(dve, high_ready, c, g, g.k + 1, "split")
                n = len(g.tiles)
                dve.tensor_tensor(
                    low[0:g.rows, g.split_slot, 0:n, :], prod_dve_v[0:g.rows, 0:n, :],
                    high[0:g.rows, g.split_slot, 0:n, :].bitcast(f32), ALU.subtract,
                ).then_inc(low_by_dve, 1)

            def products(stage, c, spread, shared, after=None):
                owed = None
                for g in groups(stage, c):
                    if g.kind == WHOLE:
                        into = prod_whole[:, g.slot, :, :]
                        if g.of_kind >= WHOLE_SLOTS:
                            wait_count(dve, products_used, c, g,
                                       WHOLES[g.of_kind - WHOLE_SLOTS].n + 1, "all")
                    elif g.kind == BY_POOL:
                        into = prod_pool[:, g.slot, :, :]
                        wait_count(dve, low_by_pool, c, g, g.of_kind - POOL_SLOTS + 1, BY_POOL)
                    else:
                        into = prod_dve_v
                        wait_count(dve, low_by_dve, c, g, g.of_kind, BY_DVE)
                    n = len(g.tiles)
                    t = slice(g.tiles[0], g.tiles[0] + n)
                    dve.tensor_tensor(
                        into[0:g.rows, 0:n, :], spread[0:g.rows, t, :],
                        shared[0:g.rows, :].unsqueeze(1).broadcast_to([g.rows, n, CN]), ALU.mult,
                    ).then_inc(products_ready, 1)
                    if owed:
                        low_parts(owed, c)
                    owed = g if g.kind == BY_DVE else None
                    if g.g == SUM_AFTER and after:
                        after()
                assert not owed

            def sum_over_d(into, src, done):
                dve.tensor_reduce(into, src[:, :].rearrange("p (b d) -> p b d", d=D),
                                  axis=AX.X, op=ALU.add).then_inc(done, 1)

            def sum_last(c, p):
                dve.wait_ge(relu_done[2], c + 1)
                sum_over_d(chunk_feats[p][:, 1, :], last, last_summed)

            def sum_direct(c, p):
                dve.wait_ge(relu_done[1], 3 * c + 3)
                if not isinstance(c, int) or c >= 2:
                    dve.wait_ge(feats_stored[p], 8 * (c - p))
                sum_over_d(chunk_feats[p][:, 0, :], direct, direct_summed)

            def copy_y(m):
                dve.wait_ge(y_done, m + 1)
                dve.tensor_copy(y_sb[:, m, :], z_y).then_inc(y_copied, 1)

            def layer0(c):
                dve.wait_ge(x0_loaded, (c + 1) * 2 * JT * 16)
                dve.wait_ge(xa_copied, c + 1)
                products(0, c, xb, xa_ps)

            def chunk(c, p):
                dve.wait_ge(xh_loaded[p], 16 * (c - p) + 32)
                dve.wait_ge(relu_done[0], 3 * c + 2)
                begun = isinstance(c, int) and c == 0
                products(1, c, xh[p], xk[0], None if begun else lambda: sum_last(c - 1, 1 - p))
                if not (isinstance(c, int) and c == CHUNKS - 1):
                    layer0(c + 1)
                dve.wait_ge(relu_done[1], 3 * c + 2)
                products(2, c, xh[p], xk[1], lambda: sum_direct(c, p))

            dve.wait_ge(staged_loaded[0], 32)
            dve.tensor_tensor(stage_sb[:, 0:T0, :], stage_sb[:, 0:T0, :],
                              stage_sb[:, TURNED:TURNED + T0, :], ALU.add).then_inc(w0_summed, 1)
            for i, g in enumerate(firsts):
                if g.split:
                    to, src = weight_tiles(g)
                    dve.wait_ge(w_rounded, i + 1)
                    dve.tensor_tensor(w_low[:, to, :], src, w_high[:, to, :].bitcast(f32),
                                      ALU.subtract).then_inc(w_ready, 1)
            dve.wait_ge(pads_cleared, 1)
            layer0(0)
            over_chunks(dve, chunk)

            def mlp_low_part(i):
                name, src = mlp_weights[i]
                dve.wait_ge(mlp_high, i + 1)
                dve.tensor_tensor(lo[name], src, hi[name].bitcast(f32),
                                  ALU.subtract).then_inc(mlp_low, 1)

            def inputs_low_parts(m):
                for i, (name, src) in enumerate(mlp_inputs(m)):
                    dve.wait_ge(inputs_high, 2 * m + i + 1)
                    dve.tensor_tensor(lo[name][m % 2], src, hi[name][m % 2].bitcast(f32),
                                      ALU.subtract).then_inc(inputs_low, 1)

            for i in range(FIRST_LAYER):
                mlp_low_part(i)
            inputs_low_parts(0)
            sum_last(CHUNKS - 1, 1)
            mlp_low_part(FIRST_LAYER)
            for m in range(MSTEPS):
                if m + 1 < MSTEPS:
                    inputs_low_parts(m + 1)
                for j in range(n1):
                    dve.wait_ge(hidden1_relu, n1 * m + j + 1)
                    if m:
                        dve.wait_ge(hidden2_done, n2 * m)
                    dve.tensor_copy(hi["h1"][:, j, :], h1[:, j, :]).then_inc(hidden1_high, 1)
                    dve.wait_ge(hidden1_high, n1 * m + j + 1)
                    dve.tensor_tensor(lo["h1"][:, j, :], h1[:, j, :], hi["h1"][:, j, :].bitcast(f32),
                                      ALU.subtract).then_inc(hidden1_low, 1)
                if m:
                    copy_y(m - 1)
            copy_y(MSTEPS - 1)

        @block.tensor
        def _(pe):
            def contract(stage, c):
                if not (isinstance(c, int) and c == 0):
                    pe.wait_ge(relu_done[stage], (1 if stage == 2 else 3) * c)
                for g in groups(stage, c):
                    def mm(weights, table, src, i, is_last=False):
                        t = g.tiles[i]
                        return pe.matmul(
                            z[stage][:, :], weights[0:g.rows, table[stage, t], :],
                            src[0:g.rows, i, :],
                            start=t == 0 and weights is not w_low and src is not lows,
                            stop=g.ends_layer and is_last)

                    every = range(len(g.tiles))
                    lows = None
                    if g.kind == WHOLE:
                        wait_count(pe, products_ready, c, g, g.n + 1, "all")
                        src = prod_whole[:, g.slot, :, :]
                        for i in every:
                            done = mm(w_whole, WHOLE_TILE, src, i, i == every[-1])
                    else:
                        wait_count(pe, high_ready, c, g, g.k + 1, "split")
                        highs = high[:, g.split_slot, :, :]
                        lows = low[:, g.split_slot, :, :]
                        for i in every:
                            mm(w_high, SPLIT_TILE, highs, i)
                            mm(w_low, SPLIT_TILE, highs, i)
                        made = low_by_pool if g.kind == BY_POOL else low_by_dve
                        wait_count(pe, made, c, g, g.of_kind + 1, g.kind)
                        for i in every:
                            done = mm(w_high, SPLIT_TILE, lows, i, i == every[-1])
                    done.then_inc(products_used, 1)

            def chunk(c, p):
                contract(1, c)
                if not (isinstance(c, int) and c == CHUNKS - 1):
                    contract(0, c + 1)
                contract(2, c)

            pe.wait_ge(w_ready, sum(g.split for g in PLAN[0, 0]))
            pe.wait_ge(w_rounded, G0)
            contract(0, 0)
            pe.wait_ge(w_ready, N_SPLIT)
            pe.wait_ge(w_rounded, N_GROUPS)
            over_chunks(pe, chunk)

            def third_layer(m):
                pe.wait_ge(hidden2_relu, n2 * (m + 1))
                if m:
                    pe.wait_ge(y_copied, m)
                for i in range(n2):
                    mm = pe.matmul(z_y, wt3[i], h2[:, i, :], start=i == 0, stop=i == n2 - 1)
                mm.then_inc(y_done, 1)

            pe.wait_ge(cols_loaded, 16)
            pe.wait_ge(mlp_high, FIRST_LAYER)
            pe.wait_ge(mlp_low, FIRST_LAYER)
            for m in range(MSTEPS):
                pe.wait_ge(inputs_high, 2 * (m + 1))
                pe.wait_ge(inputs_low, 2 * (m + 1))
                for j in range(n1):
                    if m:
                        pe.wait_ge(hidden1_relu, n1 * (m - 1) + j + 1)
                    js = slice(j * 128, (j + 1) * 128)
                    ks = [((hi["wt1"][:, i, js], lo["wt1"][:, i, js]),
                           (hi["feats"][m % 2][:, i, :], lo["feats"][m % 2][:, i, :]))
                          for i in range(2)]
                    ks.append(((hi["wt1c"][:, js], lo["wt1c"][:, js]),
                               (hi["ctx"][m % 2], lo["ctx"][m % 2])))
                    for i, ((wh, wl), (xhi, xlo)) in enumerate(ks):
                        pe.matmul(z_h1[j], wh, xhi, start=i == 0, stop=False)
                        pe.matmul(z_h1[j], wl, xhi, start=False, stop=False)
                        mm = pe.matmul(z_h1[j], wh, xlo, start=False, stop=i == 2)
                    mm.then_inc(hidden1_done, 1)
                if m:
                    third_layer(m - 1)
                    pe.wait_ge(hidden2_relu, n2 * m)
                else:
                    pe.wait_ge(mlp_high, len(mlp_weights))
                    pe.wait_ge(mlp_low, len(mlp_weights))
                for part in range(2):
                    for i in range(n1):
                        pe.wait_ge((hidden1_high, hidden1_low)[part], n1 * m + i + 1)
                        for j in range(n2):
                            js = slice(j * 128, (j + 1) * 128)
                            if part == 0:
                                pe.matmul(z_h2[j], hi["wt2"][:, i, js], hi["h1"][:, i, :],
                                          start=i == 0, stop=False)
                                pe.matmul(z_h2[j], lo["wt2"][:, i, js], hi["h1"][:, i, :],
                                          start=False, stop=False)
                            else:
                                mm = pe.matmul(z_h2[j], hi["wt2"][:, i, js], lo["h1"][:, i, :],
                                               start=False, stop=i == n1 - 1)
                                if i == n1 - 1:
                                    mm.then_inc(hidden2_done, 1)
            third_layer(MSTEPS - 1)

        @block.scalar
        def _(act):
            def layer_out(stage, c):
                end = groups(stage, c)[-1]
                wait_count(act, products_used, c, end, end.n + 1, "all")
                begun = isinstance(c, int) and c == 0
                if stage == 2:
                    if not begun:
                        act.wait_ge(last_summed, c)
                    act.activation(last[:, :], z[2][:, :], ACT.Relu,
                                   bias=bias[2]).then_inc(relu_done[2], 1)
                    return
                if not begun:
                    wait_made(act, stage + 1, c - 1)
                feed = slice(0, H) if stage == 0 else slice(H, 128)
                leave = slice(H, 128) if stage == 0 else slice(0, H)
                for half in (slice(0, H), slice(H, 128)):
                    act.activation(xk[stage][half, :], z[stage][feed, :], ACT.Relu,
                                   bias=bias[stage][feed, :]).then_inc(relu_done[stage], 1)
                if stage == 0 and not begun:
                    act.wait_ge(direct_summed, c)
                act.activation(direct[leave, :], z[stage][leave, :], ACT.Relu,
                               bias=bias[stage][leave, :]).then_inc(relu_done[stage], 1)

            def copy_xa(c):
                act.wait_ge(x0_loaded, (c + 1) * 2 * JT * 16)
                if not (isinstance(c, int) and c == 0):
                    wait_made(act, 0, c - 1)
                act.activation(xa_ps[0:JT * F, :], xa[:, :], ACT.Copy).then_inc(xa_copied, 1)

            def round_group(g, c):
                wait_count(act, products_ready, c, g, g.n + 1, "all")
                if g.k >= SPLIT_SLOTS:
                    wait_count(act, products_used, c, g, SPLITS[g.k - SPLIT_SLOTS].n + 1, "all")
                n = len(g.tiles)
                src = prod_pool[:, g.slot, :, :] if g.kind == BY_POOL else prod_dve_v
                act.activation(high[0:g.rows, g.split_slot, 0:n, :], src[0:g.rows, 0:n, :],
                               ACT.Copy).then_inc(high_ready, 1)

            def round_stage(stage, c, between=()):
                between = dict(between)
                for i, g in enumerate(g for g in groups(stage, c) if g.split):
                    round_group(g, c)
                    if i in between:
                        between[i]()

            def round_mlp(i):
                name, src = mlp_weights[i]
                act.activation(hi[name], src, ACT.Copy).then_inc(mlp_high, 1)

            def chunk(c, p):
                final = isinstance(c, int) and c == CHUNKS - 1
                begun = isinstance(c, int) and c == 0
                during1 = {}
                if not begun:
                    during1[LAST_OUT_AFTER] = lambda: layer_out(2, c - 1)
                if not final:
                    during1[XA_AFTER] = lambda: copy_xa(c + 1)
                round_stage(1, c, during1)
                if not final:
                    round_stage(0, c + 1)
                layer_out(1, c)
                if final:
                    act.wait_ge(mlp_loaded, 64)
                    for i in range(FIRST_LAYER):
                        round_mlp(i)
                round_stage(2, c, {} if final else {FIRST_OUT_AFTER: lambda: layer_out(0, c + 1)})

            act.wait_ge(w0_summed, 1)
            for g in firsts:
                if g.g == 0 and g.stage:
                    act.wait_ge(staged_loaded[g.stage], 16)
                to, src = weight_tiles(g)
                act.activation((w_high if g.split else w_whole)[:, to, :], src,
                               ACT.Copy).then_inc(w_rounded, 1)
            act.wait_ge(cols_loaded, 16)
            copy_xa(0)
            round_stage(0, 0)
            layer_out(0, 0)
            over_chunks(act, chunk)

            def round_inputs(m):
                act.wait_ge(feats_loaded[m], 16)
                if m >= 2:
                    act.wait_ge(hidden1_done, n1 * (m - 1))
                for name, src in mlp_inputs(m):
                    act.activation(hi[name][m % 2], src, ACT.Copy).then_inc(inputs_high, 1)

            def second_out(m):
                for j in range(n2):
                    act.wait_ge(hidden2_done, n2 * m + j + 1)
                    if m and j == 0:
                        act.wait_ge(y_done, m)
                    act.activation(h2[:, j, :], z_h2[j], ACT.Relu,
                                   bias=bt2[j]).then_inc(hidden2_relu, 1)

            act.wait_ge(products_used, WT2_FREE)
            round_mlp(FIRST_LAYER)
            act.wait_ge(products_used, INPUTS_FREE)
            round_inputs(0)
            layer_out(2, CHUNKS - 1)
            for m in range(MSTEPS):
                if m + 1 < MSTEPS:
                    round_inputs(m + 1)
                for j in range(n1):
                    act.wait_ge(hidden1_done, n1 * m + j + 1)
                    if m:
                        act.wait_ge(hidden1_low, n1 * (m - 1) + j + 1)
                    act.activation(h1[:, j, :], z_h1[j], ACT.Relu,
                                   bias=bt1[j]).then_inc(hidden1_relu, 1)
                second_out(m)


def kernel(**inputs):
    import concourse.bacc as bacc
    from concourse.bass_utils import run_bass_kernel_spmd

    a = {k: np.ascontiguousarray(np.asarray(v)) for k, v in inputs.items()}

    w0 = a["L0_rec_w0"]
    w0a = np.zeros((128, T0, S), w0.dtype)
    w0b = np.zeros((128, T0, S), w0.dtype)
    first = np.arange(F)
    for j in range(SHIFTS):
        second = (first + j) % F
        at = slice(j % JT * F, (j % JT + 1) * F)
        w0a[at, j // JT] = w0[first, second]
        if j:
            w0b[at, j // JT] = w0[second, first]

    def by_fields(w):
        tiles = np.zeros((2 * TK, H, w.shape[2]), w.dtype)
        tiles[:F] = w
        return np.ascontiguousarray(tiles.reshape(TK, 2 * H, w.shape[2]).transpose(1, 0, 2))

    def by_128(m):
        return np.ascontiguousarray(m.reshape(-1, 128, m.shape[1]).transpose(1, 0, 2))

    turned = np.r_[H:S, 0:H]
    wt1 = a["W_top1"]
    cols = np.concatenate(
        [a["L0_rec_b0"].reshape(1, S), a["L0_rec_b1"][turned].reshape(1, S),
         a["L0_rec_b2"].reshape(1, S), a["b_top1"].reshape(-1, 128), a["b_top2"].reshape(-1, 128),
         a["W_top3"].reshape(-1, 128)]).T
    ids = np.zeros((CHUNKS, CB, FG * GATHERS), a["ids"].dtype)
    ids[:, :, :F] = a["ids"].reshape(CHUNKS, CB, F)
    ids = ids.reshape(CHUNKS, CB, FG, GATHERS).transpose(0, 2, 1, 3).reshape(CHUNKS * 128, GATHERS)
    tables = [a[f"tbl_{f}"] for f in range(F)]
    begins = np.zeros(FG * GATHERS, a["ids"].dtype)
    begins[:F] = np.cumsum([0] + [len(t) for t in tables[:-1]])
    row_base = np.repeat(begins.reshape(FG, GATHERS), CB, axis=0)
    arrays = {
        "table": np.concatenate(tables),
        "ids": np.ascontiguousarray(ids),
        "row_base": row_base,
        "ctx_t": np.ascontiguousarray(a["dense_ctx"].T),
        "staged": np.concatenate([w0a, by_fields(a["L0_rec_w1"][:, :, turned]),
                                  by_fields(a["L0_rec_w2"]), w0b], axis=1),
        "wt1": by_128(np.concatenate([wt1[H:2 * H], wt1[0:H], wt1[2 * H:4 * H]])),
        "wt1c": np.ascontiguousarray(wt1[4 * H:]),
        "wt2": by_128(a["W_top2"]),
        "cols": np.ascontiguousarray(cols),
    }

    nc = bacc.Bacc("TRN2", target_bir_lowering=False, num_devices=1)
    dram = {k: nc.dram_tensor(k, v.shape, mybir.dt.from_np(v.dtype), kind="ExternalInput").ap()
            for k, v in arrays.items()}
    out = nc.dram_tensor("out", (B, 1), mybir.dt.float32, kind="ExternalOutput").ap()
    tower(nc, *dram.values(), out)
    r = run_bass_kernel_spmd(nc, [arrays], core_ids=[0])
    return r.results[0]["out"]
```
